# Optimizing a Trainium2 kernel written in Bass

```python
import numpy as np
import jax
import jax.numpy as jnp

def _softmax(x, axis=-1):
    return jax.nn.softmax(x, axis=axis)

def _gelu(x):
    return jax.nn.gelu(x, approximate=True)

def _silu(x):
    return jax.nn.silu(x)

def _sigmoid(x):
    return jax.nn.sigmoid(x)

def _layernorm(x, axis=-1, eps=1e-05):
    m = jnp.mean(x, axis=axis, keepdims=True)
    v = jnp.var(x, axis=axis, keepdims=True)
    return (x - m) / jnp.sqrt(v + eps)

def _scatter_add(tgt, idx, src, axis=0):
    return tgt.at[idx].add(src)

def _segment_sum(src, seg, n):
    return jax.ops.segment_sum(src, seg, n)
kernel_name = 'mk_flamingo_gated_d1_seqx_r8_1a7bbb'

def setup_inputs(seed: int=0):
    np.random.seed(seed)
    _w = jnp.asarray

    def _rec_inputs():
        import jax
        import jax.numpy as jnp
        _rk = jax.random.key(seed)
        x = -0.000125 + 0.9999 * jax.random.normal(jax.random.fold_in(_rk, 1), (16, 64, 512), jnp.float32)
        _lenS = 64 - jax.random.randint(jax.random.fold_in(_rk, 7), (16,), 0, max(1, 64 // 4) + 1, jnp.int32)
        _lenS2 = 64 - jax.random.randint(jax.random.fold_in(_rk, 8), (16,), 0, max(1, 64 // 4) + 1, jnp.int32)
        _ctx_4096P = jax.random.normal(jax.random.fold_in(_rk, 11), (16, 16, 512), jnp.float32)
        _ctx_4096c = jax.random.dirichlet(jax.random.fold_in(_rk, 511), 0.3 * jnp.ones((16,), jnp.float32), (16, 64))
        _ctx_4096t = jnp.einsum('bsk,bkd->bsd', _ctx_4096c, _ctx_4096P)
        _ctx_4096t = _ctx_4096t * jax.lax.rsqrt(jnp.mean(jnp.square(_ctx_4096t)) + 1e-12) * 0.953939
        ctx_4096 = -1.52775e-05 + 0.999936 * (_ctx_4096t + 0.3 * jax.random.normal(jax.random.fold_in(_rk, 611), (16, 64, 512), jnp.float32))
        _g = jax.random.normal(jax.random.fold_in(_rk, 9001), (2, 1), jnp.float32)
        _g = jnp.sign(_g) * jnp.maximum(jnp.abs(_g), 1.0) + (_g == 0) * 1.0
        g_xattn = _g[0]
        g_ffn = _g[1]
        return (x, ctx_4096, g_xattn, g_ffn)
    x, ctx_4096, g_xattn, g_ffn = _rec_inputs()

    def _L0_xattn_setup():
        import jax, jax.numpy as jnp
        import numpy as np
        H = 8
        C = 2

        def _autocorrelation(Q, K, V):
            B, L, D = Q.shape
            d = D // H
            q = Q.reshape(B, L, H, d).transpose(0, 2, 1, 3)
            k = K.reshape(B, L, H, d).transpose(0, 2, 1, 3)
            v = V.reshape(B, L, H, d).transpose(0, 2, 1, 3)
            qf = jnp.fft.fft(q, axis=2)
            kf = jnp.fft.fft(k, axis=2)
            corr = jnp.fft.ifft(qf * jnp.conj(kf), axis=2).real
            topk = int(C * np.log(L))
            w, idx = jax.lax.top_k(corr.transpose(0, 1, 3, 2), topk)
            w = jax.nn.softmax(w, axis=-1)
            pos = jnp.arange(L)[:, None]
            out = jnp.zeros_like(v)
            for i in range(topk):
                g = jnp.minimum(idx[:, :, None, :, i] + pos, L - 1)
                out = out + w[:, :, None, :, i] * jnp.take_along_axis(v, g, axis=2)
            return out.transpose(0, 2, 1, 3).reshape(B, L, D)
        key = jax.random.key(seed)
        k1, k2, k3 = jax.random.split(key, 3)
        B, L, D = (16, 64, 512)
        Q = jax.random.normal(k1, (B, L, D), dtype=jnp.float32)
        K = jax.random.normal(k2, (B, L, D), dtype=jnp.float32)
        V = jax.random.normal(k3, (B, L, D), dtype=jnp.float32)
        return {'Q': Q, 'K': K, 'V': V}
    _L0_xattn_all = _L0_xattn_setup()
    _L0_xattn_in = {k: v for k, v in _L0_xattn_all.items() if k in ()}
    del _L0_xattn_all

    def _L0_ffn_setup():
        import jax, jax.numpy as jnp
        import numpy as np
        HD, M = (512, 1792)
        key = jax.random.key(seed)
        k_x, k_g, k_u, k_d = jax.random.split(key, 4)
        scale = 1.0 / np.sqrt(HD)
        x = jax.random.normal(k_x, (4, 256, HD), dtype=jnp.float16)
        W_gate = jax.random.normal(k_g, (M, HD), dtype=jnp.float16) * jnp.float16(scale)
        W_up = jax.random.normal(k_u, (M, HD), dtype=jnp.float16) * jnp.float16(scale)
        W_down = jax.random.normal(k_d, (HD, M), dtype=jnp.float16) * jnp.float16(1.0 / np.sqrt(M))
        return {'x': x, 'W_gate': W_gate, 'W_up': W_up, 'W_down': W_down}
    _L0_ffn_all = _L0_ffn_setup()
    _L0_ffn_in = {k: v for k, v in _L0_ffn_all.items() if k in ('W_gate', 'W_up', 'W_down')}
    del _L0_ffn_all
    return {'x': x, 'ctx_4096': ctx_4096, 'g_xattn': g_xattn, 'g_ffn': g_ffn, 'L0_ffn_W_gate': _L0_ffn_in['W_gate'], 'L0_ffn_W_up': _L0_ffn_in['W_up'], 'L0_ffn_W_down': _L0_ffn_in['W_down']}

def reference(x, ctx_4096, g_xattn, g_ffn, L0_ffn_W_gate, L0_ffn_W_up, L0_ffn_W_down):
    import jax
    import jax.numpy as jnp

    def _L0_xattn_ref(Q, K, V):
        import jax, jax.numpy as jnp
        import numpy as np
        H = 8
        C = 2

        def _autocorrelation(Q, K, V):
            B, L, D = Q.shape
            d = D // H
            q = Q.reshape(B, L, H, d).transpose(0, 2, 1, 3)
            k = K.reshape(B, L, H, d).transpose(0, 2, 1, 3)
            v = V.reshape(B, L, H, d).transpose(0, 2, 1, 3)
            qf = jnp.fft.fft(q, axis=2)
            kf = jnp.fft.fft(k, axis=2)
            corr = jnp.fft.ifft(qf * jnp.conj(kf), axis=2).real
            topk = int(C * np.log(L))
            w, idx = jax.lax.top_k(corr.transpose(0, 1, 3, 2), topk)
            w = jax.nn.softmax(w, axis=-1)
            pos = jnp.arange(L)[:, None]
            out = jnp.zeros_like(v)
            for i in range(topk):
                g = jnp.minimum(idx[:, :, None, :, i] + pos, L - 1)
                out = out + w[:, :, None, :, i] * jnp.take_along_axis(v, g, axis=2)
            return out.transpose(0, 2, 1, 3).reshape(B, L, D)
        return _autocorrelation(Q, K, V)

    def _L0_ffn_ref(x, W_gate, W_up, W_down):
        import jax, jax.numpy as jnp
        import numpy as np
        HD, M = (512, 1792)
        gate = jnp.einsum('bsh,mh->bsm', x, W_gate)
        up = jnp.einsum('bsh,mh->bsm', x, W_up)
        h = jax.nn.silu(gate) * up
        out = jnp.einsum('bsm,hm->bsh', h, W_down)
        return out
    x = x + jnp.tanh(g_xattn[0]) * _L0_xattn_ref(_layernorm(x, axis=-1), ctx_4096, ctx_4096)
    x = x + jnp.tanh(g_ffn[0]) * _L0_ffn_ref(_layernorm(x, axis=-1), L0_ffn_W_gate, L0_ffn_W_up, L0_ffn_W_down)
    return x

_drawn_inputs = setup_inputs


def setup_inputs(seed=0):
    import zlib

    import numpy as np

    out = dict(_drawn_inputs(seed))
    spreads = {}
    factors = {}
    for name, (base, spread) in spreads.items():
        noise = np.random.default_rng([zlib.crc32(name.encode()), seed]).standard_normal(out[name].shape)
        drawn = base * np.exp(spread * noise) if base else spread * noise
        out[name] = jnp.asarray(drawn.astype(out[name].dtype))
    for name, factor in factors.items():
        out[name] = (out[name] * factor).astype(out[name].dtype)
    return out
```

```python
import numpy as np

import concourse.bass as bass
import concourse.mybir as mybir

B, L, D = 16, 64, 512
M = 1792
TOP = 8
P = 128

PAIRS = B // 2
QUADS = B // 4
QB, QP = 4, 2
KT = D // P
MT = M // P
STEPS = MT // 2
TOK = QB * L
CH = D // P
EPS = 1e-5
GONE = -3.0e38
SPEC = 1.0 / 64
MIX_UP = 8.0


def spectral_matrices():
    t = np.arange(L)
    half = L // 2

    def cos(f):
        return np.cos(2 * np.pi * np.outer(t, f) / L)

    def sin(f):
        return np.sin(2 * np.pi * np.outer(t, f) / L)

    f = np.arange(1, half)
    ends = cos(np.array([0, half]))
    last = np.zeros((L, 2))
    last[-1, 0] = 1.0
    plain = np.hstack([ends, cos(f), -sin(f)])
    swapped = np.hstack([last, -sin(f), cos(f)])
    even = np.hstack([plain, plain])
    even_kv = np.hstack([plain, swapped])

    g = np.arange(half) + 0.5
    odd = np.hstack([cos(g), -sin(g), cos(g), -sin(g)])
    odd_v = np.hstack([cos(g), -sin(g), -sin(g), cos(g)])
    odd_v[-1] -= odd_v.sum(0)

    none = np.zeros((2, L))
    lags = np.vstack([ends.T, 2 * cos(f).T, 2 * cos(f).T, none, 2 * sin(f).T, -2 * sin(f).T])
    lags *= 1 / (L * SPEC)
    mix_last = np.zeros((2, L))
    mix_last[0] = L
    mix_even = np.vstack([ends.T, 2 * cos(f).T, 2 * cos(f).T, mix_last, -2 * sin(f).T, 2 * sin(f).T])
    mix_odd = np.vstack([2 * cos(g).T, 2 * cos(g).T, -2 * sin(g).T, 2 * sin(g).T])
    return even, even_kv, odd, odd_v, lags, mix_even, mix_odd


MIX_SCALE = 1.0 / (2 * L * SPEC * MIX_UP)

FORWARD = ("even_kv", "odd_v", "even", "odd")
LAG0 = len(FORWARD) * 2 * P
MIX0 = LAG0 + 2 * L
MIXW = 3 * L
CONSTS = MIX0 + 4 * MIXW


def constant_table():
    even, even_kv, odd, odd_v, lags, mix_even, mix_odd = spectral_matrices()
    table = np.zeros((P, CONSTS), np.float16)

    def parts(m):
        high = m.astype(np.float16)
        return high, (m - high).astype(np.float16)

    for n, m in enumerate((even_kv, odd_v, even, odd)):
        for part, v in enumerate(parts(m)):
            col = (2 * n + part) * P
            table[:, col:col + P] = np.vstack([v, v])
    for part, v in enumerate(parts(lags)):
        table[:, LAG0 + part * L:LAG0 + (part + 1) * L] = v
    for n, m in enumerate((mix_even, mix_odd)):
        for part, v in enumerate(parts(m)):
            col = MIX0 + (2 * n + part) * MIXW
            table[:, col + L:col + 2 * L] = v
    return table


def attention_and_ffn_order():
    A = [("stats", 0), ("stats", 1), ("split", 0), ("split", 1),
         "F", ("spectra", 0), ("spectra", 1), "F", ("psplit", 0), ("spectra", 2), ("psplit", 1),
         ("spectra", 3), ("psplit", 2), ("psplit", 3), "F",
         ("lags", 0), ("lags", 1), ("exp", 0), "F", ("lags", 2), ("exp", 1), ("mask", 0), ("lags", 3),
         ("exp", 2), ("mask", 1), ("exp", 3), "F", ("wt", 0), ("mask", 2), ("wt", 1), ("mask", 3), "F",
         ("wt", 2), ("wspec", 0), ("wt", 3), "F", ("p2split", 0), ("wspec", 1), "F",
         ("wspec", 2), ("p2split", 1), ("wspec", 3), ("mix", 0), ("p2split", 2), "F", ("p2split", 3), ("xn", 0),
         ("mix", 1), "F", ("xt", 0), ("xn", 1), "F", ("xt", 1), "F"]
    F = []
    for s in range(STEPS):
        F.append([("gate_up", s)] + ([("hidden", s - 1)] if s else []) + ([("hsplit", s - 2)] if s > 1 else []))
    F.append([("hidden", STEPS - 1), ("hsplit", STEPS - 2)])
    F[-1] += [("hsplit", STEPS - 1)]
    F += [[("down", (0, 0))], [("down", (0, 1)), ("out", 0)], [("down", (1, 0))], [("down", (1, 1)), ("out", 1)]]
    slots = A.count("F")
    assert slots == len(F), (slots, len(F))
    attention, ffn, both = [], [], []
    n = 0
    for a in A:
        if a == "F":
            ffn += F[n]
            both += F[n]
            n += 1
        else:
            attention.append(a)
            both.append(a)
    return attention, ffn, both


def build(nc, x, ctx, g_xattn, g_ffn, w_gate, w_up, w_down, table, eye, out):
    f32, f16 = mybir.dt.float32, mybir.dt.float16
    ALU = mybir.AluOpType
    ACT = mybir.ActivationFunctionType
    AX = mybir.AxisListType

    def sb(name, shape, dt=f32):
        return nc.alloc_sbuf_tensor(name, shape, dt)

    x_sb = sb("x_sb", [P, PAIRS, D])
    ctx_sb = sb("ctx_sb", [P, PAIRS, D])
    wg = sb("wg", [P, KT, M], f16)
    wu = sb("wu", [P, KT, M], f16)
    wd = sb("wd", [P, MT, D], f16)
    consts = sb("consts", [P, CONSTS], f16)
    ident = sb("ident", [P, P])
    minus_half = sb("minus_half", [P, 1])
    gates = sb("gates", [P, 2])
    gates_tanh = sb("gates_tanh", [P, 2])
    scales = sb("scales", [P, 2])

    raw_stats = sb("raw_stats", [P, 2 * QP, 6])
    mean_var = sb("mean_var", [P, 2 * QP, 2])
    var_eps = sb("var_eps", [P, 2 * QP])
    rstd = sb("rstd", [P, 2 * QP])

    q32 = sb("q32", [P, QP, D])
    k_stack = sb("k_stack", [P, QB, D], f16)
    q_stack = sb("q_stack", [P, QB, D], f16)
    kv_spec = sb("kv_spec", [P, QB, 2, D])
    prod = sb("prod", [P, 2, D])
    prod_hi = sb("prod_hi", [P, QB, D], f16)
    prod_lo = sb("prod_lo", [P, QB, D], f16)
    top8 = sb("top8", [P, QB, CH, TOP])
    rest = sb("rest", [P, QB, CH, L])
    expo = sb("expo", [P, QB, CH, L + TOP])
    total = sb("total", [P, QB, CH])
    inv_total = sb("inv_total", [P, QB, CH])
    probs = sb("probs", [P, QB, CH, L])
    w_stack = sb("w_stack", [P, QB, D], f16)
    mixed = sb("mixed", [P, 2, 2, D])
    mixed_hi = sb("mixed_hi", [P, QB, 2, D], f16)
    mixed_lo = sb("mixed_lo", [P, QB, 2, D], f16)

    xn = sb("xn", [P, QP, D])
    xt_hi = sb("xt_hi", [P, KT, TOK], f16)
    xt_lo = sb("xt_lo", [P, KT, TOK], f16)
    act32 = sb("act32", [P, 2, 2 * TOK])
    hid32 = sb("hid32", [P, 2, 2 * TOK])
    hid_hi = sb("hid_hi", [P, MT, TOK], f16)
    hid_lo = sb("hid_lo", [P, MT, TOK], f16)

    psum = nc.alloc_psum_tensor("psum", [P, 8, 512], f32)

    S = {}

    def sem(name):
        S[name] = nc.alloc_semaphore(name)
        return S[name]

    x_first, x_more = sem("x_first"), sem("x_more")
    ctx_first, ctx_more = sem("ctx_first"), sem("ctx_more")
    forward_loaded, small_loaded = sem("forward_loaded"), sem("small_loaded")
    gate_loaded, up_loaded, down_loaded = sem("gate_loaded"), sem("up_loaded"), sem("down_loaded")
    const_set = sem("const_set")
    tanh_gates, scales_ready = sem("tanh_gates"), sem("scales_ready")
    raw1, stats1, eps1, rstd1 = sem("raw1"), sem("stats1"), sem("eps1"), sem("rstd1")
    raw2, stats2, eps2, rstd2 = sem("raw2"), sem("stats2"), sem("eps2"), sem("rstd2")
    k_high, k_low = sem("k_high"), sem("k_low")
    q_ready, q_high, q_low = sem("q_ready"), sem("q_high"), sem("q_low")
    kv_spectra, q_spectra, kv_copied = sem("kv_spectra"), sem("q_spectra"), sem("kv_copied")
    prod_done, prod_high, prod_low = sem("prod_done"), sem("prod_high"), sem("prod_low")
    lags_done, top8_done, logits_ready = sem("lags_done"), sem("top8_done"), sem("logits_ready")
    exp_done, sum_done, inv_ready = sem("exp_done"), sem("sum_done"), sem("inv_ready")
    exp_scaled, probs_ready = sem("exp_scaled"), sem("probs_ready")
    wt_done, w_high, w_low = sem("wt_done"), sem("w_high"), sem("w_low")
    w_spectra = sem("w_spectra")
    mixed_done, mixed_high, mixed_low = sem("mixed_done"), sem("mixed_high"), sem("mixed_low")
    mix_done, x1_ready = sem("mix_done"), sem("x1_ready")
    xn_ready, xt_done, xt_high, xt_low = sem("xn_ready"), sem("xt_done"), sem("xt_high"), sem("xt_low")
    gate_up_done, tanh_done, silu_done = sem("gate_up_done"), sem("tanh_done"), sem("silu_done")
    hid_done, hid_high, hid_low = sem("hid_done"), sem("hid_high"), sem("hid_low")
    down_done, out_ready, stored = sem("down_done"), sem("out_ready"), sem("stored")

    attention, ffn, both = attention_and_ffn_order()

    def alone(engine, always_met, count):
        if not isinstance(count, int):
            engine.to_reg(count)
        engine.wait_ge(always_met, 16)

    def forward(name, part):
        col = (2 * FORWARD.index(name) + part) * P
        return consts[:, col:col + P]

    def mix_matrix(n, part, half):
        col = MIX0 + (2 * n + part) * MIXW + (L if half == 0 else 0)
        return consts[:, col:col + P]

    def rows(half):
        return slice(half * L, (half + 1) * L)

    def one(tile, partitions, n):
        return tile[partitions, bass.ds(n, 1), :].rearrange("p a d -> p (a d)")

    with nc.Block() as block:

        @block.sync
        def _(sp):
            xv = x.rearrange("(n p) d -> p n d", p=P)
            cv = ctx.rearrange("(n p) d -> p n d", p=P)
            sp.dma_start(x_sb[:, 0:QP, :], xv[:, 0:QP, :]).then_inc(x_first, 16)
            sp.dma_start(consts[:, :], table).then_inc(forward_loaded, 16)
            sp.dma_start(wg[:, :, :], w_gate).then_inc(gate_loaded, 16)
            sp.dma_start(x_sb[:, QP:PAIRS, :], xv[:, QP:PAIRS, :]).then_inc(x_more, 16)
            sp.dma_start(wd[:, :, :], w_down).then_inc(down_loaded, 16)
            outv = out.rearrange("(n p) d -> p n d", p=P)

            with sp.Fori(0, PAIRS) as n:
                sp.wait_ge(out_ready, n + 2)
                sp.dma_start(outv[:, bass.ds(n, 1), :], x_sb[:, bass.ds(n, 1), :]).then_inc(stored, 16)
            sp.wait_ge(stored, 16 * PAIRS)

        @block.gpsimd
        def _(pool):
            nc.gpsimd.memset(minus_half[:, :], -0.5).then_inc(const_set, 1)
            pool.wait_ge(const_set, 1)

            def reciprocal_std(n, stats_done, eps_done, rstd_done, count):
                alone(pool, x_first, count)
                pool.wait_ge(stats_done, count)
                nc.gpsimd.tensor_scalar_add(var_eps[:, n:n + 1], mean_var[:, n, 1:2], EPS).then_inc(eps_done, 1)
                pool.wait_ge(eps_done, count)
                nc.gpsimd.tensor_tensor(rstd[:, n:n + 1], var_eps[:, n:n + 1], minus_half[:, :],
                                        ALU.pow).then_inc(rstd_done, 1)

            def attention_step(step, n, i):
                if step == "stats":
                    reciprocal_std(n, stats1, eps1, rstd1, QP * i + n + 1)
                if step == "psplit":
                    pool.wait_ge(prod_high, QB * i + n + 1)
                    nc.gpsimd.tensor_tensor(prod_lo[:, n, :], prod[:, n % 2, :], prod_hi[:, n, :],
                                            ALU.subtract).then_inc(prod_low, 1)
                if step == "exp":
                    pool.wait_ge(inv_ready, QB * i + n + 1)
                    nc.gpsimd.tensor_tensor(expo[:, n, :, 0:L], expo[:, n, :, 0:L],
                                            inv_total[:, n, :].unsqueeze(2).broadcast_to([P, CH, L]),
                                            ALU.mult).then_inc(exp_scaled, 1)
                if step == "p2split":
                    pool.wait_ge(mixed_high, QB * i + n + 1)
                    nc.gpsimd.tensor_tensor(mixed_lo[:, n, :, :], mixed[:, n % 2, :, :], mixed_hi[:, n, :, :],
                                            ALU.subtract).then_inc(mixed_low, 1)
                if step == "mix":
                    reciprocal_std(QP + n, stats2, eps2, rstd2, QP * i + n + 1)

            def ffn_step(step, n, j):
                if step == "hsplit":
                    pool.wait_ge(hid_high, STEPS * j + n + 1)
                    nc.gpsimd.tensor_tensor(hid_lo[:, 2 * n:2 * n + 2, :].rearrange("p a t -> p (a t)"),
                                            hid32[:, n % 2, :],
                                            hid_hi[:, 2 * n:2 * n + 2, :].rearrange("p a t -> p (a t)"),
                                            ALU.subtract).then_inc(hid_low, 1)

            for step, n in attention:
                attention_step(step, n, 0)
            with pool.Fori(1, QUADS) as i:
                for step, n in both:
                    attention_step(step, n, i)
                    ffn_step(step, n, i - 1)
            for step, n in ffn:
                ffn_step(step, n, QUADS - 1)

        @block.scalar
        def _(act):
            act.dma_start(ctx_sb[:, 0:QP, :], ctx.rearrange("(n p) d -> p n d", p=P)[:, 0:QP, :])\
               .then_inc(ctx_first, 16)
            act.dma_start(gates[:, 0:1], g_xattn).then_inc(small_loaded, 16)
            act.dma_start(gates[:, 1:2], g_ffn).then_inc(small_loaded, 16)
            act.dma_start(ident[:, :], eye).then_inc(small_loaded, 16)
            act.dma_start(wu[:, :, :], w_up).then_inc(up_loaded, 16)
            act.dma_start(ctx_sb[:, QP:PAIRS, :], ctx.rearrange("(n p) d -> p n d", p=P)[:, QP:PAIRS, :])\
               .then_inc(ctx_more, 16)
            act.wait_ge(small_loaded, 48)
            nc.scalar.activation(gates_tanh[:, :], gates[:, :], ACT.Tanh).then_inc(tanh_gates, 1)

            def attention_step(step, n, i, first):
                if step == "split":
                    if not first and n == 0:
                        act.wait_ge(kv_spectra, QB * i)
                        act.wait_ge(q_spectra, QB * i)
                    for h in range(2):
                        last = nc.scalar.activation(k_stack[rows(h), 2 * n + h, :],
                                                    one(ctx_sb, rows(h), QP * i + n), ACT.Copy)
                    last.then_inc(k_high, 1)
                    act.wait_ge(q_ready, QP * i + n + 1)
                    for h in range(2):
                        last = nc.scalar.activation(q_stack[rows(h), 2 * n + h, :], q32[rows(h), n, :], ACT.Copy)
                    last.then_inc(q_high, 1)
                if step == "spectra":
                    act.wait_ge(kv_spectra, QB * i + n + 1)
                    if not first and n == 0:
                        act.wait_ge(mixed_done, QB * i)
                    nc.scalar.activation(kv_spec[:, n, :, :], psum[:, 4:6, :], ACT.Copy,
                                         scale=SPEC).then_inc(kv_copied, 1)
                if step == "psplit":
                    act.wait_ge(prod_done, QB * i + n + 1)
                    if not first and n == 0:
                        act.wait_ge(lags_done, QB * i)
                    nc.scalar.activation(prod_hi[:, n, :], prod[:, n % 2, :], ACT.Copy).then_inc(prod_high, 1)
                if step == "exp":
                    act.wait_ge(logits_ready, QB * i + n + 1)
                    nc.scalar.activation(expo[:, n, :, :], expo[:, n, :, :], ACT.Exp).then_inc(exp_done, 1)
                if step == "wt":
                    act.wait_ge(wt_done, QB * i + n + 1)
                    if not first and n == 0:
                        act.wait_ge(w_spectra, QB * i)
                    nc.scalar.activation(w_stack[0:L, n, :], psum[0:L, 4 + n, :], ACT.Copy).then_inc(w_high, 1)
                if step == "p2split":
                    act.wait_ge(mixed_done, QB * i + n + 1)
                    if not first and n == 0:
                        act.wait_ge(mix_done, QP * i)
                    nc.scalar.activation(mixed_hi[:, n, :, :], mixed[:, n % 2, :, :], ACT.Copy)\
                      .then_inc(mixed_high, 1)
                if step == "xt":
                    act.wait_ge(xt_done, QP * i + n + 1)
                    if not first:
                        act.wait_ge(gate_up_done, STEPS * i)
                    nc.scalar.activation(xt_hi[:, :, n * P:(n + 1) * P],
                                         psum[:, 6 + n, :].rearrange("p (k t) -> p k t", k=KT),
                                         ACT.Copy).then_inc(xt_high, 1)

            def ffn_step(step, n, j):
                if step == "gate_up":
                    act.wait_ge(gate_up_done, STEPS * j + n + 1)
                    nc.scalar.activation(act32[:, n % 2, :], psum[:, 2 * (n % 2), :], ACT.Tanh,
                                         scale=0.5).then_inc(tanh_done, 1)
                if step == "hsplit":
                    act.wait_ge(hid_done, STEPS * j + n + 1)
                    nc.scalar.activation(hid_hi[:, 2 * n:2 * n + 2, :].rearrange("p a t -> p (a t)"),
                                         hid32[:, n % 2, :], ACT.Copy).then_inc(hid_high, 1)

            act.wait_ge(ctx_first, 16)
            for step, n in attention:
                attention_step(step, n, 0, True)
            act.wait_ge(ctx_more, 16)
            with act.Fori(1, QUADS) as i:
                for step, n in both:
                    attention_step(step, n, i, False)
                    ffn_step(step, n, i - 1)
            for step, n in ffn:
                ffn_step(step, n, QUADS - 1)

        @block.vector
        def _(dve):
            def layer_stats(n, pair, raw_done, stats_done, count):
                nc.vector.bn_stats(raw_stats[:, n, :], one(x_sb, slice(0, P), pair)).then_inc(raw_done, 1)
                alone(dve, x_first, count)
                dve.wait_ge(raw_done, count)
                nc.vector.bn_aggr(mean_var[:, n, :], raw_stats[:, n, :]).then_inc(stats_done, 1)

            def attention_step(step, n, i, first):
                if step == "stats":
                    layer_stats(n, QP * i + n, raw1, stats1, QP * i + n + 1)
                if step == "split":
                    dve.wait_ge(rstd1, QP * i + n + 1)
                    nc.vector.tensor_scalar(q32[:, n, :], one(x_sb, slice(0, P), QP * i + n),
                                            mean_var[:, n, 0:1], rstd[:, n:n + 1],
                                            ALU.subtract, ALU.mult).then_inc(q_ready, 1)
                    dve.wait_ge(k_high, QP * i + n + 1)
                    for h in range(2):
                        last = nc.vector.tensor_tensor(k_stack[rows(1 - h), 2 * n + h, :],
                                                       one(ctx_sb, rows(h), QP * i + n),
                                                       k_stack[rows(h), 2 * n + h, :], ALU.subtract)
                    last.then_inc(k_low, 1)
                    dve.wait_ge(q_high, QP * i + n + 1)
                    for h in range(2):
                        last = nc.vector.tensor_tensor(q_stack[rows(1 - h), 2 * n + h, :], q32[rows(h), n, :],
                                                       q_stack[rows(h), 2 * n + h, :], ALU.subtract)
                    last.then_inc(q_low, 1)
                if step == "spectra":
                    dve.wait_ge(q_spectra, QB * i + n + 1)
                    dve.wait_ge(kv_copied, QB * i + n + 1)
                    if n >= 2:
                        dve.wait_ge(prod_low, QB * i + n - 1)
                    elif not first:
                        dve.wait_ge(prod_low, QB * i)
                    nc.vector.tensor_tensor(prod[:, n % 2, :], psum[:, 6 + n % 2, :], kv_spec[:, n, 0, :],
                                            ALU.mult).then_inc(prod_done, 1)
                if step == "lags":
                    alone(dve, x_first, QB * i + n + 1)
                    dve.wait_ge(lags_done, QB * i + n + 1)
                    corr = psum[:, 4 + n, 0:CH * L].rearrange("p (c l) -> p c l", c=CH)
                    for c in range(CH):
                        last = nc.vector.max(top8[:, n, c, :], corr[:, c, :])
                    last.then_inc(top8_done, 1)
                    alone(dve, x_first, QB * i + n + 1)
                    dve.wait_ge(top8_done, QB * i + n + 1)
                    for c in range(CH):
                        nc.vector.match_replace(rest[:, n, c, :], top8[:, n, c, :], corr[:, c, :], GONE)
                    nc.vector.tensor_tensor(expo[:, n, :, 0:L], corr,
                                            top8[:, n, :, 0:1].broadcast_to([P, CH, L]), ALU.subtract)
                    nc.vector.tensor_tensor(expo[:, n, :, L:L + TOP], top8[:, n, :, :],
                                            top8[:, n, :, 0:1].broadcast_to([P, CH, TOP]),
                                            ALU.subtract).then_inc(logits_ready, 1)
                if step == "exp":
                    dve.wait_ge(exp_done, QB * i + n + 1)
                    nc.vector.tensor_reduce(total[:, n, :], expo[:, n, :, L:L + TOP], AX.X,
                                            ALU.add).then_inc(sum_done, 1)
                    dve.wait_ge(sum_done, QB * i + n + 1)
                    nc.vector.reciprocal(inv_total[:, n, :], total[:, n, :]).then_inc(inv_ready, 1)
                if step == "mask":
                    dve.wait_ge(exp_scaled, QB * i + n + 1)
                    if not first and n == 0:
                        dve.wait_ge(wt_done, QB * i)
                    nc.vector.scalar_tensor_tensor(probs[:, n, :, :], rest[:, n, :, :], GONE,
                                                   expo[:, n, :, 0:L], ALU.is_equal,
                                                   ALU.mult).then_inc(probs_ready, 1)
                if step == "wt":
                    dve.wait_ge(w_high, QB * i + n + 1)
                    nc.vector.tensor_tensor(w_stack[L:P, n, :], psum[0:L, 4 + n, :], w_stack[0:L, n, :],
                                            ALU.subtract).then_inc(w_low, 1)
                if step == "wspec":
                    dve.wait_ge(w_spectra, QB * i + n + 1)
                    if n >= 2:
                        dve.wait_ge(mixed_low, QB * i + n - 1)
                    elif not first:
                        dve.wait_ge(mixed_low, QB * i)
                    bank = 4 + 2 * (n % 2)
                    nc.vector.scalar_tensor_tensor(mixed[:, n % 2, :, :], psum[:, bank:bank + 2, :], MIX_UP,
                                                   kv_spec[:, n, :, :], ALU.mult,
                                                   ALU.mult).then_inc(mixed_done, 1)
                if step == "mix":
                    dve.wait_ge(mix_done, QP * i + n + 1)
                    tokens = one(x_sb, slice(0, P), QP * i + n)
                    nc.vector.scalar_tensor_tensor(tokens, psum[:, 4 + n, :], scales[:, 0:1], tokens,
                                                   ALU.mult, ALU.add).then_inc(x1_ready, 1)
                    alone(dve, x_first, QP * i + n + 1)
                    dve.wait_ge(x1_ready, QP * i + n + 1)
                    layer_stats(QP + n, QP * i + n, raw2, stats2, QP * i + n + 1)
                if step == "xn":
                    dve.wait_ge(rstd2, QP * i + n + 1)
                    if not first:
                        dve.wait_ge(xt_done, QP * i)
                    nc.vector.tensor_scalar(xn[:, n, :], one(x_sb, slice(0, P), QP * i + n),
                                            mean_var[:, QP + n, 0:1], rstd[:, QP + n:QP + n + 1],
                                            ALU.subtract, ALU.mult).then_inc(xn_ready, 1)
                if step == "xt":
                    dve.wait_ge(xt_high, QP * i + n + 1)
                    nc.vector.tensor_tensor(xt_lo[:, :, n * P:(n + 1) * P],
                                            psum[:, 6 + n, :].rearrange("p (k t) -> p k t", k=KT),
                                            xt_hi[:, :, n * P:(n + 1) * P], ALU.subtract).then_inc(xt_low, 1)

            def ffn_step(step, n, j):
                if step == "hidden":
                    gate, up = psum[:, 2 * (n % 2), :], psum[:, 2 * (n % 2) + 1, :]
                    a = act32[:, n % 2, :]
                    dve.wait_ge(tanh_done, STEPS * j + n + 1)
                    nc.vector.scalar_tensor_tensor(a, a, 1.0, gate, ALU.add, ALU.mult).then_inc(silu_done, 1)
                    dve.wait_ge(silu_done, STEPS * j + n + 1)
                    if n >= 2:
                        dve.wait_ge(hid_low, STEPS * j + n - 1)
                    nc.vector.tensor_tensor(hid32[:, n % 2, :], a, up, ALU.mult).then_inc(hid_done, 1)
                if step == "out":
                    dve.wait_ge(down_done, QP * j + n + 1)
                    tokens = one(x_sb, slice(0, P), QP * j + n)
                    nc.vector.scalar_tensor_tensor(tokens, psum[:, 2 + n, :], scales[:, 1:2], tokens,
                                                   ALU.mult, ALU.add).then_inc(out_ready, 1)

            dve.wait_ge(tanh_gates, 1)
            nc.vector.tensor_scalar(scales[:, 0:1], gates_tanh[:, 0:1], MIX_SCALE, None, ALU.mult)\
              .then_inc(out_ready, 1)
            nc.vector.tensor_scalar(scales[:, 1:2], gates_tanh[:, 1:2], 0.5, None, ALU.mult)\
              .then_inc(scales_ready, 1)
            dve.wait_ge(x_first, 16)
            dve.wait_ge(ctx_first, 16)
            dve.wait_ge(scales_ready, 1)
            for step, n in attention:
                attention_step(step, n, 0, True)
            dve.wait_ge(x_more, 16)
            with dve.Fori(1, QUADS) as i:
                for step, n in both:
                    attention_step(step, n, i, False)
                    ffn_step(step, n, i - 1)
            for step, n in ffn:
                ffn_step(step, n, QUADS - 1)

        @block.tensor
        def _(pe):
            def transform(bank, name, stack):
                for part in range(2):
                    last = nc.tensor.matmul(psum[:, bank, :], forward(name, part), stack,
                                            start=(part == 0), stop=(part == 1))
                return last

            def attention_step(step, n, i, first):
                if step == "spectra":
                    pe.wait_ge(k_low, QP * i + n // 2 + 1)
                    if n >= 1:
                        pe.wait_ge(kv_copied, QB * i + n)
                    elif not first:
                        pe.wait_ge(x1_ready, QP * i)
                    transform(4, "even_kv", k_stack[:, n, :])
                    transform(5, "odd_v", k_stack[:, n, :]).then_inc(kv_spectra, 1)
                    pe.wait_ge(q_low, QP * i + n // 2 + 1)
                    if n >= 2:
                        pe.wait_ge(prod_done, QB * i + n - 1)
                    elif not first:
                        pe.wait_ge(xt_low, QP * i)
                    transform(6 + n % 2, "even", q_stack[:, n, :]).then_inc(q_spectra, 1)
                if step == "lags":
                    if n == 0:
                        pe.wait_ge(prod_done, QB * i + QB)
                    pe.wait_ge(prod_low, QB * i + n + 1)
                    for c in range(CH):
                        o = psum[:, 4 + n, c * L:(c + 1) * L]
                        high = prod_hi[:, n, c * P:(c + 1) * P]
                        low = prod_lo[:, n, c * P:(c + 1) * P]
                        nc.tensor.matmul(o, high, consts[:, LAG0:LAG0 + L], start=True, stop=False)
                        nc.tensor.matmul(o, high, consts[:, LAG0 + L:LAG0 + 2 * L], start=False, stop=False)
                        last = nc.tensor.matmul(o, low, consts[:, LAG0:LAG0 + L], start=False, stop=True)
                    last.then_inc(lags_done, 1)
                if step == "wt":
                    alone(pe, forward_loaded, QB * i + n + 1)
                    pe.wait_ge(probs_ready, QB * i + n + 1)
                    for c in range(CH):
                        last = nc.tensor.transpose(psum[0:L, 4 + n, c * P:(c + 1) * P], probs[:, n, c, :],
                                                   ident[:, :])
                    last.then_inc(wt_done, 1)
                if step == "wspec":
                    bank = 4 + 2 * (n % 2)
                    if n < 2:
                        pe.wait_ge(w_low, QB * i + 2 * n + 2)
                    else:
                        pe.wait_ge(w_low, QB * i + n + 1)
                        pe.wait_ge(mixed_done, QB * i + n - 1)
                    transform(bank, "even", w_stack[:, n, :])
                    transform(bank + 1, "odd", w_stack[:, n, :]).then_inc(w_spectra, 1)
                if step == "mix":
                    pe.wait_ge(mixed_low, QB * i + 2 * n + 2)
                    pe.wait_ge(mixed_done, QB * i + 3)
                    todo = [(h, m, a, b) for h in range(2) for m in range(2) for a, b in ((0, 0), (1, 0), (0, 1))]
                    for at, (h, m, a, b) in enumerate(todo):
                        data = (mixed_hi, mixed_lo)[b][:, 2 * n + h, m, :]
                        last = nc.tensor.matmul(psum[:, 4 + n, :], mix_matrix(m, a, h), data,
                                                start=(at == 0), stop=(at == len(todo) - 1))
                    last.then_inc(mix_done, 1)
                if step == "xt":
                    pe.wait_ge(xn_ready, QP * i + n + 1)
                    pe.wait_ge(mixed_done, QB * i + QB)
                    for k in range(KT):
                        last = nc.tensor.transpose(psum[:, 6 + n, k * P:(k + 1) * P],
                                                   xn[:, n, k * P:(k + 1) * P], ident[:, :])
                    last.then_inc(xt_done, 1)

            def ffn_step(step, n, j):
                if step == "gate_up":
                    if n == 0:
                        pe.wait_ge(xt_low, QP * j + QP)
                    elif n == 1:
                        pe.wait_ge(out_ready, QP * j + 1)
                    else:
                        pe.wait_ge(hid_done, STEPS * j + n - 1)
                    for w, bank in ((wg, 2 * (n % 2)), (wu, 2 * (n % 2) + 1)):
                        for a in range(2):
                            m = (2 * n + a) * P
                            for k in range(KT):
                                for part, xt in enumerate((xt_hi, xt_lo)):
                                    last = nc.tensor.matmul(psum[:, bank, a * TOK:(a + 1) * TOK],
                                                            w[:, k, m:m + P], xt[:, k, :],
                                                            start=(k == 0 and part == 0),
                                                            stop=(k == KT - 1 and part == 1))
                    last.then_inc(gate_up_done, 1)
                if step == "down":
                    p, part_of = n
                    if part_of == 0:
                        pe.wait_ge(hid_low, STEPS * j + STEPS)
                    tok = slice(p * P, (p + 1) * P)
                    half = MT // 2
                    for m in range(part_of * half, (part_of + 1) * half):
                        for part, hid in enumerate((hid_hi, hid_lo)):
                            last = nc.tensor.matmul(psum[:, 2 + p, :], hid[:, m, tok], wd[:, m, :],
                                                    start=(m == 0 and part == 0),
                                                    stop=(m == MT - 1 and part == 1))
                    if part_of == 1:
                        last.then_inc(down_done, 1)

            pe.wait_ge(forward_loaded, 16)
            pe.wait_ge(small_loaded, 48)
            for step, n in attention:
                attention_step(step, n, 0, True)
            pe.wait_ge(gate_loaded, 16)
            pe.wait_ge(up_loaded, 16)
            pe.wait_ge(down_loaded, 16)
            with pe.Fori(1, QUADS) as i:
                for step, n in both:
                    attention_step(step, n, i, False)
                    ffn_step(step, n, i - 1)
            for step, n in ffn:
                ffn_step(step, n, QUADS - 1)


def kernel(**inputs):
    import concourse.bacc as bacc
    from concourse.bass_utils import run_bass_kernel_spmd

    def tiles(w, contract):
        return np.ascontiguousarray(np.asarray(w).T.reshape(contract, P, -1).transpose(1, 0, 2))

    arrays = {
        "x": np.ascontiguousarray(np.asarray(inputs["x"]).reshape(B * L, D)),
        "ctx": np.ascontiguousarray(np.asarray(inputs["ctx_4096"]).reshape(B * L, D)),
        "g_xattn": np.ascontiguousarray(np.broadcast_to(np.asarray(inputs["g_xattn"]).reshape(1, 1), (P, 1))),
        "g_ffn": np.ascontiguousarray(np.broadcast_to(np.asarray(inputs["g_ffn"]).reshape(1, 1), (P, 1))),
        "w_gate": tiles(inputs["L0_ffn_W_gate"], KT),
        "w_up": tiles(inputs["L0_ffn_W_up"], KT),
        "w_down": tiles(inputs["L0_ffn_W_down"], MT),
        "table": constant_table(),
        "eye": np.eye(P, dtype=np.float32),
    }
    nc = bacc.Bacc("TRN2", target_bir_lowering=False, num_devices=1)
    args = [nc.dram_tensor(n, a.shape, mybir.dt.from_np(a.dtype), kind="ExternalInput").ap()
            for n, a in arrays.items()]
    out = nc.dram_tensor("out", (B * L, D), mybir.dt.float32, kind="ExternalOutput").ap()
    build(nc, *args, out)
    r = run_bass_kernel_spmd(nc, [arrays], core_ids=[0])
    return r.results[0]["out"].reshape(B, L, D)
```

```python
import numpy as np

import concourse.bass as bass
import concourse.mybir as mybir

B, L, D = 16, 64, 512
M = 1792
TOP = 8
P = 128

PAIRS = B // 2
QUADS = B // 4
QB, QP = 4, 2
KT = D // P
MT = M // P
STEPS = MT // 2
TOK = QB * L
CH = D // P
EPS = 1e-5
GONE = -3.0e38
SPEC = 1.0 / 64
MIX_UP = 8.0


def spectral_matrices():
    t = np.arange(L)
    half = L // 2

    def cos(f):
        return np.cos(2 * np.pi * np.outer(t, f) / L)

    def sin(f):
        return np.sin(2 * np.pi * np.outer(t, f) / L)

    f = np.arange(1, half)
    ends = cos(np.array([0, half]))
    last = np.zeros((L, 2))
    last[-1, 0] = 1.0
    plain = np.hstack([ends, cos(f), -sin(f)])
    swapped = np.hstack([last, -sin(f), cos(f)])
    even = np.hstack([plain, plain])
    even_kv = np.hstack([plain, swapped])

    g = np.arange(half) + 0.5
    odd = np.hstack([cos(g), -sin(g), cos(g), -sin(g)])
    odd_v = np.hstack([cos(g), -sin(g), -sin(g), cos(g)])
    odd_v[-1] -= odd_v.sum(0)

    none = np.zeros((2, L))
    lags = np.vstack([ends.T, 2 * cos(f).T, 2 * cos(f).T, none, 2 * sin(f).T, -2 * sin(f).T])
    lags *= 1 / (L * SPEC)
    mix_last = np.zeros((2, L))
    mix_last[0] = L
    mix_even = np.vstack([ends.T, 2 * cos(f).T, 2 * cos(f).T, mix_last, -2 * sin(f).T, 2 * sin(f).T])
    mix_odd = np.vstack([2 * cos(g).T, 2 * cos(g).T, -2 * sin(g).T, 2 * sin(g).T])
    return even, even_kv, odd, odd_v, lags, mix_even, mix_odd


MIX_SCALE = 1.0 / (2 * L * SPEC * MIX_UP)

FORWARD = ("even_kv", "odd_v", "even", "odd")
LAG0 = len(FORWARD) * 2 * P
MIX0 = LAG0 + 2 * L
MIXW = 3 * L
CONSTS = MIX0 + 4 * MIXW


def constant_table():
    even, even_kv, odd, odd_v, lags, mix_even, mix_odd = spectral_matrices()
    table = np.zeros((P, CONSTS), np.float16)

    def parts(m):
        high = m.astype(np.float16)
        return high, (m - high).astype(np.float16)

    for n, m in enumerate((even_kv, odd_v, even, odd)):
        for part, v in enumerate(parts(m)):
            col = (2 * n + part) * P
            table[:, col:col + P] = np.vstack([v, v])
    for part, v in enumerate(parts(lags)):
        table[:, LAG0 + part * L:LAG0 + (part + 1) * L] = v
    for n, m in enumerate((mix_even, mix_odd)):
        for part, v in enumerate(parts(m)):
            col = MIX0 + (2 * n + part) * MIXW
            table[:, col + L:col + 2 * L] = v
    return table


DOWN_PARTS = ((0, 4), (4, 8), (8, 11), (11, 14))


def attention_and_ffn_order():
    A = [("stats", 0), ("stats", 1), "F", ("split", 0), "F", ("split", 1), "F", ("spectra", 0), "F", ("spectra", 1),
         ("psplit", 0), "F", ("spectra", 2), ("psplit", 1), "F", ("spectra", 3), ("psplit", 2), "F",
         ("psplit", 3), ("lags", 0), ("lags", 1), "F", ("exp", 0), ("lags", 2), ("exp", 1), "F", ("mask", 0),
         ("lags", 3), ("exp", 2), ("mask", 1), "F", ("exp", 3), ("wt", 0), ("mask", 2), "F",
         ("wt", 1), ("mask", 3), "F", ("wspec", 0), ("wt", 2), "F", ("wspec", 1), ("p2split", 0), ("wt", 3),
         "F", ("wspec", 2), ("p2split", 1), "F", ("wspec", 3), ("p2split", 2), "F", ("mix", 0), ("p2split", 3),
         "F", ("xn", 0), "F", ("xt", 0), "F", ("mix", 1), "F", ("xn", 1), ("xt", 1), "F", "F"]
    F = []
    for s in range(STEPS):
        F.append([("gate", s)] + ([("hsplit", s - 2)] if s > 1 else []))
        F.append([("up", s)] + ([("hidden", s - 1)] if s else []))
    parts = len(DOWN_PARTS)
    F += [[("down", (p, part))] + ([("out", p)] if part == parts - 1 else [])
          for p in range(QP) for part in range(parts)]
    n = 2 * STEPS
    F[n] = [("hidden", STEPS - 1), ("hsplit", STEPS - 2)] + F[n] + [("hsplit", STEPS - 1)]
    assert A.count("F") == len(F), (A.count("F"), len(F))
    attention, ffn, both = [], [], []
    n = 0
    for a in A:
        if a == "F":
            ffn += F[n]
            both += F[n]
            n += 1
        else:
            attention.append(a)
            both.append(a)
    return attention, ffn, both


def build(nc, x, ctx, g_xattn, g_ffn, w_gate, w_up, w_down, table, eye, out):
    f32, f16 = mybir.dt.float32, mybir.dt.float16
    ALU = mybir.AluOpType
    ACT = mybir.ActivationFunctionType
    AX = mybir.AxisListType

    def sb(name, shape, dt=f32):
        return nc.alloc_sbuf_tensor(name, shape, dt)

    x_sb = sb("x_sb", [P, PAIRS, D])
    ctx_sb = sb("ctx_sb", [P, PAIRS, D])
    wg = sb("wg", [P, KT, M], f16)
    wu = sb("wu", [P, KT, M], f16)
    wd = sb("wd", [P, MT, D], f16)
    consts = sb("consts", [P, CONSTS], f16)
    ident = sb("ident", [P, P])
    minus_half = sb("minus_half", [P, 1])
    gates = sb("gates", [P, 2])
    gates_tanh = sb("gates_tanh", [P, 2])
    scales = sb("scales", [P, 2])

    raw_stats = sb("raw_stats", [P, 2 * QP, 6])
    mean_var = sb("mean_var", [P, 2 * QP, 2])
    var_eps = sb("var_eps", [P, 2 * QP])
    rstd = sb("rstd", [P, 2 * QP])

    q32 = sb("q32", [P, QP, D])
    k_stack = sb("k_stack", [P, QB, D], f16)
    q_stack = sb("q_stack", [P, QB, D], f16)
    kv_spec = sb("kv_spec", [P, QB, 2, D])
    prod = sb("prod", [P, 2, D])
    prod_hi = sb("prod_hi", [P, QB, D], f16)
    prod_lo = sb("prod_lo", [P, QB, D], f16)
    top8 = sb("top8", [P, QB, CH, TOP])
    rest = sb("rest", [P, QB, CH, L])
    expo = sb("expo", [P, QB, CH, L + TOP])
    total = sb("total", [P, QB, CH])
    inv_total = sb("inv_total", [P, QB, CH])
    probs = sb("probs", [P, QB, CH, L])
    w_stack = sb("w_stack", [P, QB, D], f16)
    mixed = sb("mixed", [P, 2, 2, D])
    mixed_hi = sb("mixed_hi", [P, QB, 2, D], f16)
    mixed_lo = sb("mixed_lo", [P, QB, 2, D], f16)

    xn = sb("xn", [P, QP, D])
    xt_hi = sb("xt_hi", [P, KT, TOK], f16)
    xt_lo = sb("xt_lo", [P, KT, TOK], f16)
    act32 = sb("act32", [P, 2, 2 * TOK])
    hid32 = sb("hid32", [P, 2, 2 * TOK])
    hid_hi = sb("hid_hi", [P, MT, TOK], f16)
    hid_lo = sb("hid_lo", [P, MT, TOK], f16)

    psum = nc.alloc_psum_tensor("psum", [P, 8, 512], f32)

    S = {}

    def sem(name):
        S[name] = nc.alloc_semaphore(name)
        return S[name]

    x_first, x_more = sem("x_first"), sem("x_more")
    ctx_first, ctx_more = sem("ctx_first"), sem("ctx_more")
    forward_loaded, small_loaded = sem("forward_loaded"), sem("small_loaded")
    inverse_loaded = sem("inverse_loaded")
    gate_loaded, up_loaded, down_loaded = sem("gate_loaded"), sem("up_loaded"), sem("down_loaded")
    const_set = sem("const_set")
    tanh_gates = sem("tanh_gates")
    raw1, stats1, eps1, rstd1 = sem("raw1"), sem("stats1"), sem("eps1"), sem("rstd1")
    raw2, stats2, eps2, rstd2 = sem("raw2"), sem("stats2"), sem("eps2"), sem("rstd2")
    k_high, k_low = sem("k_high"), sem("k_low")
    q_ready, q_high, q_low = sem("q_ready"), sem("q_high"), sem("q_low")
    k_spectra, v_spectra, q_spectra = sem("k_spectra"), sem("v_spectra"), sem("q_spectra")
    k_copied, v_copied = sem("k_copied"), sem("v_copied")
    prod_done, prod_high, prod_low = sem("prod_done"), sem("prod_high"), sem("prod_low")
    lags_done, top8_done, logits_ready = sem("lags_done"), sem("top8_done"), sem("logits_ready")
    exp_done, sum_done, inv_ready = sem("exp_done"), sem("sum_done"), sem("inv_ready")
    exp_scaled, probs_ready = sem("exp_scaled"), sem("probs_ready")
    wt_done, w_high, w_low = sem("wt_done"), sem("w_high"), sem("w_low")
    w_spectra = sem("w_spectra")
    mixed_done, mixed_high, mixed_low = sem("mixed_done"), sem("mixed_high"), sem("mixed_low")
    mix_done, x1_ready = sem("mix_done"), sem("x1_ready")
    xn_ready, xt_done, xt_high, xt_low = sem("xn_ready"), sem("xt_done"), sem("xt_high"), sem("xt_low")
    gate_done, up_done, tanh_done, silu_done = sem("gate_done"), sem("up_done"), sem("tanh_done"), sem("silu_done")
    hid_done, hid_high, hid_low = sem("hid_done"), sem("hid_high"), sem("hid_low")
    down_done, out_ready, stored = sem("down_done"), sem("out_ready"), sem("stored")

    attention, ffn, both = attention_and_ffn_order()

    def alone(engine, always_met, count):
        if not isinstance(count, int):
            engine.to_reg(count)
        engine.wait_ge(always_met, 16)

    def forward(name, part):
        col = (2 * FORWARD.index(name) + part) * P
        return consts[:, col:col + P]

    def mix_matrix(n, part, half):
        col = MIX0 + (2 * n + part) * MIXW + (L if half == 0 else 0)
        return consts[:, col:col + P]

    def rows(half):
        return slice(half * L, (half + 1) * L)

    def one(tile, partitions, n):
        return tile[partitions, bass.ds(n, 1), :].rearrange("p a d -> p (a d)")

    with nc.Block() as block:

        @block.sync
        def _(sp):
            xv = x.rearrange("(n p) d -> p n d", p=P)
            cv = ctx.rearrange("(n p) d -> p n d", p=P)
            sp.dma_start(x_sb[:, 0:QP, :], xv[:, 0:QP, :]).then_inc(x_first, 16)
            sp.dma_start(consts[:, 0:LAG0], table[:, 0:LAG0]).then_inc(forward_loaded, 16)
            sp.dma_start(consts[:, LAG0:CONSTS], table[:, LAG0:CONSTS]).then_inc(inverse_loaded, 16)
            sp.dma_start(wg[:, :, :], w_gate).then_inc(gate_loaded, 16)
            sp.dma_start(x_sb[:, QP:PAIRS, :], xv[:, QP:PAIRS, :]).then_inc(x_more, 16)
            sp.dma_start(ctx_sb[:, QP:PAIRS, :], cv[:, QP:PAIRS, :]).then_inc(ctx_more, 16)
            sp.dma_start(wu[:, :, :], w_up).then_inc(up_loaded, 16)
            sp.dma_start(wd[:, :, :], w_down).then_inc(down_loaded, 16)
            outv = out.rearrange("(n p) d -> p n d", p=P)

            with sp.Fori(0, PAIRS) as n:
                sp.wait_ge(out_ready, n + 2)
                sp.dma_start(outv[:, bass.ds(n, 1), :], x_sb[:, bass.ds(n, 1), :]).then_inc(stored, 16)
            sp.wait_ge(stored, 16 * PAIRS)

        @block.gpsimd
        def _(pool):
            nc.gpsimd.memset(minus_half[:, :], -0.5).then_inc(const_set, 1)
            pool.wait_ge(const_set, 1)

            def reciprocal_std(n, stats_done, eps_done, rstd_done, count):
                alone(pool, x_first, count)
                pool.wait_ge(stats_done, count)
                nc.gpsimd.tensor_scalar_add(var_eps[:, n:n + 1], mean_var[:, n, 1:2], EPS).then_inc(eps_done, 1)
                pool.wait_ge(eps_done, count)
                nc.gpsimd.tensor_tensor(rstd[:, n:n + 1], var_eps[:, n:n + 1], minus_half[:, :],
                                        ALU.pow).then_inc(rstd_done, 1)

            def attention_step(step, n, i):
                if step == "stats":
                    reciprocal_std(n, stats1, eps1, rstd1, QP * i + n + 1)
                if step == "psplit":
                    pool.wait_ge(prod_high, QB * i + n + 1)
                    nc.gpsimd.tensor_tensor(prod_lo[:, n, :], prod[:, n % 2, :], prod_hi[:, n, :],
                                            ALU.subtract).then_inc(prod_low, 1)
                if step == "exp":
                    pool.wait_ge(inv_ready, QB * i + n + 1)
                    nc.gpsimd.tensor_tensor(expo[:, n, :, 0:L], expo[:, n, :, 0:L],
                                            inv_total[:, n, :].unsqueeze(2).broadcast_to([P, CH, L]),
                                            ALU.mult).then_inc(exp_scaled, 1)
                if step == "p2split":
                    pool.wait_ge(mixed_high, QB * i + n + 1)
                    nc.gpsimd.tensor_tensor(mixed_lo[:, n, :, :], mixed[:, n % 2, :, :], mixed_hi[:, n, :, :],
                                            ALU.subtract).then_inc(mixed_low, 1)
                if step == "mix":
                    reciprocal_std(QP + n, stats2, eps2, rstd2, QP * i + n + 1)

            def ffn_step(step, n, j):
                if step == "hsplit":
                    pool.wait_ge(hid_high, STEPS * j + n + 1)
                    nc.gpsimd.tensor_tensor(hid_lo[:, 2 * n:2 * n + 2, :].rearrange("p a t -> p (a t)"),
                                            hid32[:, n % 2, :],
                                            hid_hi[:, 2 * n:2 * n + 2, :].rearrange("p a t -> p (a t)"),
                                            ALU.subtract).then_inc(hid_low, 1)

            for step, n in attention:
                attention_step(step, n, 0)
            with pool.Fori(1, QUADS) as i:
                for step, n in both:
                    attention_step(step, n, i)
                    ffn_step(step, n, i - 1)
            for step, n in ffn:
                ffn_step(step, n, QUADS - 1)

        @block.scalar
        def _(act):
            act.dma_start(ctx_sb[:, 0:QP, :], ctx.rearrange("(n p) d -> p n d", p=P)[:, 0:QP, :])\
               .then_inc(ctx_first, 16)
            act.dma_start(gates[:, 0:1], g_xattn).then_inc(small_loaded, 16)
            act.dma_start(gates[:, 1:2], g_ffn).then_inc(small_loaded, 16)
            act.dma_start(ident[:, :], eye).then_inc(small_loaded, 16)

            def attention_step(step, n, i, first):
                if step == "split":
                    if not first and n == 0:
                        act.wait_ge(v_spectra, QB * i)
                        act.wait_ge(q_spectra, QB * i)
                    for h in range(2):
                        last = nc.scalar.activation(k_stack[rows(h), 2 * n + h, :],
                                                    one(ctx_sb, rows(h), QP * i + n), ACT.Copy)
                    last.then_inc(k_high, 1)
                    act.wait_ge(q_ready, QP * i + n + 1)
                    for h in range(2):
                        last = nc.scalar.activation(q_stack[rows(h), 2 * n + h, :], q32[rows(h), n, :], ACT.Copy)
                    last.then_inc(q_high, 1)
                if step == "spectra":
                    act.wait_ge(k_spectra, QB * i + n + 1)
                    if not first and n == 0:
                        act.wait_ge(mixed_done, QB * i)
                    nc.scalar.activation(kv_spec[:, n, 0, :], psum[:, 4, :], ACT.Copy,
                                         scale=SPEC).then_inc(k_copied, 1)
                    act.wait_ge(v_spectra, QB * i + n + 1)
                    nc.scalar.activation(kv_spec[:, n, 1, :], psum[:, 5, :], ACT.Copy,
                                         scale=SPEC).then_inc(v_copied, 1)
                if step == "psplit":
                    act.wait_ge(prod_done, QB * i + n + 1)
                    if not first and n == 0:
                        act.wait_ge(lags_done, QB * i)
                    nc.scalar.activation(prod_hi[:, n, :], prod[:, n % 2, :], ACT.Copy).then_inc(prod_high, 1)
                if step == "exp":
                    if first and n == 0:
                        act.wait_ge(small_loaded, 48)
                        nc.scalar.activation(gates_tanh[:, :], gates[:, :], ACT.Tanh).then_inc(tanh_gates, 1)
                    act.wait_ge(logits_ready, QB * i + n + 1)
                    nc.scalar.activation(expo[:, n, :, :], expo[:, n, :, :], ACT.Exp).then_inc(exp_done, 1)
                if step == "wt":
                    act.wait_ge(wt_done, QB * i + n + 1)
                    if not first and n == 0:
                        act.wait_ge(w_spectra, QB * i)
                    nc.scalar.activation(w_stack[0:L, n, :], psum[0:L, 4 + n % 2, :],
                                         ACT.Copy).then_inc(w_high, 1)
                if step == "p2split":
                    act.wait_ge(mixed_done, QB * i + n + 1)
                    if not first and n == 0:
                        act.wait_ge(mix_done, QP * i)
                    nc.scalar.activation(mixed_hi[:, n, :, :], mixed[:, n % 2, :, :], ACT.Copy)\
                      .then_inc(mixed_high, 1)
                if step == "xt":
                    act.wait_ge(xt_done, QP * i + n + 1)
                    if not first:
                        act.wait_ge(up_done, STEPS * i)
                    nc.scalar.activation(xt_hi[:, :, n * P:(n + 1) * P],
                                         psum[:, 6 + n, :].rearrange("p (k t) -> p k t", k=KT),
                                         ACT.Copy).then_inc(xt_high, 1)

            def ffn_step(step, n, j):
                if step == "gate":
                    act.wait_ge(gate_done, STEPS * j + n + 1)
                    nc.scalar.activation(act32[:, n % 2, :], psum[:, 2 * (n % 2), :], ACT.Tanh,
                                         scale=0.5).then_inc(tanh_done, 1)
                if step == "hsplit":
                    act.wait_ge(hid_done, STEPS * j + n + 1)
                    nc.scalar.activation(hid_hi[:, 2 * n:2 * n + 2, :].rearrange("p a t -> p (a t)"),
                                         hid32[:, n % 2, :], ACT.Copy).then_inc(hid_high, 1)

            act.wait_ge(ctx_first, 16)
            for step, n in attention:
                attention_step(step, n, 0, True)
            act.wait_ge(ctx_more, 16)
            with act.Fori(1, QUADS) as i:
                for step, n in both:
                    attention_step(step, n, i, False)
                    ffn_step(step, n, i - 1)
            for step, n in ffn:
                ffn_step(step, n, QUADS - 1)

        @block.vector
        def _(dve):
            def layer_stats(n, pair, raw_done, stats_done, count):
                nc.vector.bn_stats(raw_stats[:, n, :], one(x_sb, slice(0, P), pair)).then_inc(raw_done, 1)
                alone(dve, x_first, count)
                dve.wait_ge(raw_done, count)
                nc.vector.bn_aggr(mean_var[:, n, :], raw_stats[:, n, :]).then_inc(stats_done, 1)

            def attention_step(step, n, i, first):
                if step == "stats":
                    layer_stats(n, QP * i + n, raw1, stats1, QP * i + n + 1)
                if step == "split":
                    dve.wait_ge(rstd1, QP * i + n + 1)
                    nc.vector.tensor_scalar(q32[:, n, :], one(x_sb, slice(0, P), QP * i + n),
                                            mean_var[:, n, 0:1], rstd[:, n:n + 1],
                                            ALU.subtract, ALU.mult).then_inc(q_ready, 1)
                    dve.wait_ge(k_high, QP * i + n + 1)
                    for h in range(2):
                        last = nc.vector.tensor_tensor(k_stack[rows(1 - h), 2 * n + h, :],
                                                       one(ctx_sb, rows(h), QP * i + n),
                                                       k_stack[rows(h), 2 * n + h, :], ALU.subtract)
                    last.then_inc(k_low, 1)
                    dve.wait_ge(q_high, QP * i + n + 1)
                    for h in range(2):
                        last = nc.vector.tensor_tensor(q_stack[rows(1 - h), 2 * n + h, :], q32[rows(h), n, :],
                                                       q_stack[rows(h), 2 * n + h, :], ALU.subtract)
                    last.then_inc(q_low, 1)
                if step == "spectra":
                    dve.wait_ge(q_spectra, QB * i + n + 1)
                    dve.wait_ge(k_copied, QB * i + n + 1)
                    if n >= 2:
                        dve.wait_ge(prod_low, QB * i + n - 1)
                    elif not first:
                        dve.wait_ge(prod_low, QB * i)
                    nc.vector.tensor_tensor(prod[:, n % 2, :], psum[:, 6 + n % 2, :], kv_spec[:, n, 0, :],
                                            ALU.mult).then_inc(prod_done, 1)
                if step == "lags":
                    alone(dve, x_first, QB * i + n + 1)
                    dve.wait_ge(lags_done, QB * i + n + 1)
                    corr = psum[:, 4 + n, 0:CH * L].rearrange("p (c l) -> p c l", c=CH)
                    for c in range(CH):
                        last = nc.vector.max(top8[:, n, c, :], corr[:, c, :])
                    last.then_inc(top8_done, 1)
                    alone(dve, x_first, QB * i + n + 1)
                    dve.wait_ge(top8_done, QB * i + n + 1)
                    for c in range(CH):
                        nc.vector.match_replace(rest[:, n, c, :], top8[:, n, c, :], corr[:, c, :], GONE)
                    nc.vector.tensor_tensor(expo[:, n, :, 0:L], corr,
                                            top8[:, n, :, 0:1].broadcast_to([P, CH, L]), ALU.subtract)
                    nc.vector.tensor_tensor(expo[:, n, :, L:L + TOP], top8[:, n, :, :],
                                            top8[:, n, :, 0:1].broadcast_to([P, CH, TOP]),
                                            ALU.subtract).then_inc(logits_ready, 1)
                if step == "exp":
                    dve.wait_ge(exp_done, QB * i + n + 1)
                    nc.vector.tensor_reduce(total[:, n, :], expo[:, n, :, L:L + TOP], AX.X,
                                            ALU.add).then_inc(sum_done, 1)
                    dve.wait_ge(sum_done, QB * i + n + 1)
                    nc.vector.reciprocal(inv_total[:, n, :], total[:, n, :]).then_inc(inv_ready, 1)
                if step == "mask":
                    dve.wait_ge(exp_scaled, QB * i + n + 1)
                    if not first and n == 0:
                        dve.wait_ge(wt_done, QB * i)
                    nc.vector.scalar_tensor_tensor(probs[:, n, :, :], rest[:, n, :, :], GONE,
                                                   expo[:, n, :, 0:L], ALU.is_equal,
                                                   ALU.mult).then_inc(probs_ready, 1)
                if step == "wt":
                    dve.wait_ge(w_high, QB * i + n + 1)
                    nc.vector.tensor_tensor(w_stack[L:P, n, :], psum[0:L, 4 + n % 2, :], w_stack[0:L, n, :],
                                            ALU.subtract).then_inc(w_low, 1)
                if step == "wspec":
                    dve.wait_ge(w_spectra, QB * i + n + 1)
                    if n >= 2:
                        dve.wait_ge(mixed_low, QB * i + n - 1)
                    elif not first:
                        dve.wait_ge(mixed_low, QB * i)
                    nc.vector.scalar_tensor_tensor(mixed[:, n % 2, :, :], psum[:, 6:8, :], MIX_UP,
                                                   kv_spec[:, n, :, :], ALU.mult,
                                                   ALU.mult).then_inc(mixed_done, 1)
                if step == "mix":
                    if first and n == 0:
                        dve.wait_ge(tanh_gates, 1)
                        nc.vector.tensor_scalar(scales[:, 0:1], gates_tanh[:, 0:1], MIX_SCALE, None, ALU.mult)
                        nc.vector.tensor_scalar(scales[:, 1:2], gates_tanh[:, 1:2], 0.5, None, ALU.mult)\
                          .then_inc(out_ready, 1)
                        dve.wait_ge(out_ready, 1)
                    dve.wait_ge(mix_done, QP * i + n + 1)
                    tokens = one(x_sb, slice(0, P), QP * i + n)
                    nc.vector.scalar_tensor_tensor(tokens, psum[:, 4 + n, :], scales[:, 0:1], tokens,
                                                   ALU.mult, ALU.add).then_inc(x1_ready, 1)
                    alone(dve, x_first, QP * i + n + 1)
                    dve.wait_ge(x1_ready, QP * i + n + 1)
                    layer_stats(QP + n, QP * i + n, raw2, stats2, QP * i + n + 1)
                if step == "xn":
                    dve.wait_ge(rstd2, QP * i + n + 1)
                    if not first:
                        dve.wait_ge(xt_done, QP * i)
                    nc.vector.tensor_scalar(xn[:, n, :], one(x_sb, slice(0, P), QP * i + n),
                                            mean_var[:, QP + n, 0:1], rstd[:, QP + n:QP + n + 1],
                                            ALU.subtract, ALU.mult).then_inc(xn_ready, 1)
                if step == "xt":
                    dve.wait_ge(xt_high, QP * i + n + 1)
                    nc.vector.tensor_tensor(xt_lo[:, :, n * P:(n + 1) * P],
                                            psum[:, 6 + n, :].rearrange("p (k t) -> p k t", k=KT),
                                            xt_hi[:, :, n * P:(n + 1) * P], ALU.subtract).then_inc(xt_low, 1)

            def ffn_step(step, n, j):
                if step == "hidden":
                    gate, up = psum[:, 2 * (n % 2), :], psum[:, 2 * (n % 2) + 1, :]
                    a = act32[:, n % 2, :]
                    dve.wait_ge(tanh_done, STEPS * j + n + 1)
                    nc.vector.scalar_tensor_tensor(a, a, 1.0, gate, ALU.add, ALU.mult).then_inc(silu_done, 1)
                    dve.wait_ge(silu_done, STEPS * j + n + 1)
                    dve.wait_ge(up_done, STEPS * j + n + 1)
                    if n >= 2:
                        dve.wait_ge(hid_low, STEPS * j + n - 1)
                    nc.vector.tensor_tensor(hid32[:, n % 2, :], a, up, ALU.mult).then_inc(hid_done, 1)
                if step == "out":
                    dve.wait_ge(down_done, QP * j + n + 1)
                    tokens = one(x_sb, slice(0, P), QP * j + n)
                    nc.vector.scalar_tensor_tensor(tokens, psum[:, 2 + n, :], scales[:, 1:2], tokens,
                                                   ALU.mult, ALU.add).then_inc(out_ready, 1)

            dve.wait_ge(x_first, 16)
            dve.wait_ge(ctx_first, 16)
            for step, n in attention:
                attention_step(step, n, 0, True)
            dve.wait_ge(x_more, 16)
            with dve.Fori(1, QUADS) as i:
                for step, n in both:
                    attention_step(step, n, i, False)
                    ffn_step(step, n, i - 1)
            for step, n in ffn:
                ffn_step(step, n, QUADS - 1)

        @block.tensor
        def _(pe):
            def transform(bank, name, stack):
                for part in range(2):
                    last = nc.tensor.matmul(psum[:, bank, :], forward(name, part), stack,
                                            start=(part == 0), stop=(part == 1))
                return last

            def attention_step(step, n, i, first):
                if step == "spectra":
                    pe.wait_ge(k_low, QP * i + n // 2 + 1)
                    if n >= 1:
                        pe.wait_ge(k_copied, QB * i + n)
                    elif not first:
                        pe.wait_ge(x1_ready, QP * i)
                    transform(4, "even_kv", k_stack[:, n, :]).then_inc(k_spectra, 1)
                    pe.wait_ge(q_low, QP * i + n // 2 + 1)
                    if n >= 2:
                        pe.wait_ge(prod_done, QB * i + n - 1)
                    elif not first:
                        pe.wait_ge(xt_low, QP * i)
                    transform(6 + n % 2, "even", q_stack[:, n, :]).then_inc(q_spectra, 1)
                    if n >= 1:
                        pe.wait_ge(v_copied, QB * i + n)
                    transform(5, "odd_v", k_stack[:, n, :]).then_inc(v_spectra, 1)
                if step == "lags":
                    if n == 0:
                        pe.wait_ge(prod_done, QB * i + QB)
                        pe.wait_ge(v_copied, QB * i + QB)
                        if first:
                            pe.wait_ge(inverse_loaded, 16)
                    pe.wait_ge(prod_low, QB * i + n + 1)
                    for c in range(CH):
                        o = psum[:, 4 + n, c * L:(c + 1) * L]
                        high = prod_hi[:, n, c * P:(c + 1) * P]
                        low = prod_lo[:, n, c * P:(c + 1) * P]
                        nc.tensor.matmul(o, high, consts[:, LAG0:LAG0 + L], start=True, stop=False)
                        nc.tensor.matmul(o, high, consts[:, LAG0 + L:LAG0 + 2 * L], start=False, stop=False)
                        last = nc.tensor.matmul(o, low, consts[:, LAG0:LAG0 + L], start=False, stop=True)
                    last.then_inc(lags_done, 1)
                if step == "wt":
                    alone(pe, forward_loaded, QB * i + n + 1)
                    pe.wait_ge(probs_ready, QB * i + n + 1)
                    if n >= 2:
                        pe.wait_ge(w_low, QB * i + n - 1)
                    if first and n == 0:
                        pe.wait_ge(small_loaded, 48)
                    for c in range(CH):
                        last = nc.tensor.transpose(psum[0:L, 4 + n % 2, c * P:(c + 1) * P], probs[:, n, c, :],
                                                   ident[:, :])
                    last.then_inc(wt_done, 1)
                if step == "wspec":
                    pe.wait_ge(w_low, QB * i + n + 1)
                    if n == 0:
                        pe.wait_ge(logits_ready, QB * i + QB)
                    else:
                        pe.wait_ge(mixed_done, QB * i + n)
                    transform(6, "even", w_stack[:, n, :])
                    transform(7, "odd", w_stack[:, n, :]).then_inc(w_spectra, 1)
                if step == "mix":
                    pe.wait_ge(w_low, QB * i + QB)
                    for part, data, done in ((0, mixed_hi, mixed_high), (1, mixed_lo, mixed_low)):
                        for h in range(2):
                            pe.wait_ge(done, QB * i + 2 * n + h + 1)
                            for m in range(2):
                                for matrix_part in ((0, 1), (0,))[part]:
                                    last = nc.tensor.matmul(psum[:, 4 + n, :], mix_matrix(m, matrix_part, h),
                                                            data[:, 2 * n + h, m, :],
                                                            start=(part + h + m + matrix_part == 0),
                                                            stop=(part + h + m == 3))
                    last.then_inc(mix_done, 1)
                if step == "xt":
                    pe.wait_ge(xn_ready, QP * i + n + 1)
                    pe.wait_ge(mixed_done, QB * i + QB)
                    for k in range(KT):
                        last = nc.tensor.transpose(psum[:, 6 + n, k * P:(k + 1) * P],
                                                   xn[:, n, k * P:(k + 1) * P], ident[:, :])
                    last.then_inc(xt_done, 1)

            def ffn_step(step, n, j):
                if step == "gate" or step == "up":
                    if step == "gate":
                        if n == 0:
                            pe.wait_ge(xt_low, QP * j + QP)
                        elif n == 1:
                            pe.wait_ge(out_ready, QP * j + 1)
                        else:
                            pe.wait_ge(hid_done, STEPS * j + n - 1)
                    w, bank = (wg, 2 * (n % 2)) if step == "gate" else (wu, 2 * (n % 2) + 1)
                    for a in range(2):
                        m = (2 * n + a) * P
                        for k in range(KT):
                            for part, xt in enumerate((xt_hi, xt_lo)):
                                last = nc.tensor.matmul(psum[:, bank, a * TOK:(a + 1) * TOK],
                                                        w[:, k, m:m + P], xt[:, k, :],
                                                        start=(k == 0 and part == 0),
                                                        stop=(k == KT - 1 and part == 1))
                    last.then_inc(gate_done if step == "gate" else up_done, 1)
                if step == "down":
                    p, part_of = n
                    tok = slice(p * P, (p + 1) * P)
                    first_m, end_m = DOWN_PARTS[part_of]
                    if p == 0 and part_of == 0:
                        pe.wait_ge(hid_done, STEPS * j + STEPS - 1)
                    if p == 0:
                        pe.wait_ge(hid_low, STEPS * j + (end_m + 1) // 2)
                    for m in range(first_m, end_m):
                        for part, hid in enumerate((hid_hi, hid_lo)):
                            last = nc.tensor.matmul(psum[:, 2 + p, :], hid[:, m, tok], wd[:, m, :],
                                                    start=(m == 0 and part == 0),
                                                    stop=(m == MT - 1 and part == 1))
                    if end_m == MT:
                        last.then_inc(down_done, 1)

            pe.wait_ge(forward_loaded, 16)
            for step, n in attention:
                attention_step(step, n, 0, True)
            pe.wait_ge(gate_loaded, 16)
            pe.wait_ge(up_loaded, 16)
            pe.wait_ge(down_loaded, 16)
            with pe.Fori(1, QUADS) as i:
                for step, n in both:
                    attention_step(step, n, i, False)
                    ffn_step(step, n, i - 1)
            for step, n in ffn:
                ffn_step(step, n, QUADS - 1)


def kernel(**inputs):
    import concourse.bacc as bacc
    from concourse.bass_utils import run_bass_kernel_spmd

    def tiles(w, contract):
        return np.ascontiguousarray(np.asarray(w).T.reshape(contract, P, -1).transpose(1, 0, 2))

    arrays = {
        "x": np.ascontiguousarray(np.asarray(inputs["x"]).reshape(B * L, D)),
        "ctx": np.ascontiguousarray(np.asarray(inputs["ctx_4096"]).reshape(B * L, D)),
        "g_xattn": np.ascontiguousarray(np.broadcast_to(np.asarray(inputs["g_xattn"]).reshape(1, 1), (P, 1))),
        "g_ffn": np.ascontiguousarray(np.broadcast_to(np.asarray(inputs["g_ffn"]).reshape(1, 1), (P, 1))),
        "w_gate": tiles(inputs["L0_ffn_W_gate"], KT),
        "w_up": tiles(inputs["L0_ffn_W_up"], KT),
        "w_down": tiles(inputs["L0_ffn_W_down"], MT),
        "table": constant_table(),
        "eye": np.eye(P, dtype=np.float32),
    }
    nc = bacc.Bacc("TRN2", target_bir_lowering=False, num_devices=1)
    args = [nc.dram_tensor(n, a.shape, mybir.dt.from_np(a.dtype), kind="ExternalInput").ap()
            for n, a in arrays.items()]
    out = nc.dram_tensor("out", (B * L, D), mybir.dt.float32, kind="ExternalOutput").ap()
    build(nc, *args, out)
    r = run_bass_kernel_spmd(nc, [arrays], core_ids=[0])
    return r.results[0]["out"].reshape(B, L, D)
```

```python
import numpy as np

import concourse.bass as bass
import concourse.mybir as mybir

B, L, D = 16, 64, 512
M = 1792
TOP = 8
P = 128

PAIRS = B // 2
QUADS = B // 4
QB, QP = 4, 2
KT = D // P
MT = M // P
STEPS = MT // 2
TOK = QB * L
CH = D // P
EPS = 1e-5
GONE = -3.0e38
SPEC = 1.0 / 64
MIX_UP = 8.0


def spectral_matrices():
    t = np.arange(L)
    half = L // 2

    def cos(f):
        return np.cos(2 * np.pi * np.outer(t, f) / L)

    def sin(f):
        return np.sin(2 * np.pi * np.outer(t, f) / L)

    f = np.arange(1, half)
    ends = cos(np.array([0, half]))
    last = np.zeros((L, 2))
    last[-1, 0] = 1.0
    plain = np.hstack([ends, cos(f), -sin(f)])
    swapped = np.hstack([last, -sin(f), cos(f)])
    even = np.hstack([plain, plain])
    even_kv = np.hstack([plain, swapped])

    g = np.arange(half) + 0.5
    odd = np.hstack([cos(g), -sin(g), cos(g), -sin(g)])
    odd_v = np.hstack([cos(g), -sin(g), -sin(g), cos(g)])
    odd_v[-1] -= odd_v.sum(0)

    none = np.zeros((2, L))
    lags = np.vstack([ends.T, 2 * cos(f).T, 2 * cos(f).T, none, 2 * sin(f).T, -2 * sin(f).T])
    lags *= 1 / (L * SPEC)
    mix_last = np.zeros((2, L))
    mix_last[0] = L
    mix_even = np.vstack([ends.T, 2 * cos(f).T, 2 * cos(f).T, mix_last, -2 * sin(f).T, 2 * sin(f).T])
    mix_odd = np.vstack([2 * cos(g).T, 2 * cos(g).T, -2 * sin(g).T, 2 * sin(g).T])
    return even, even_kv, odd, odd_v, lags, mix_even, mix_odd


MIX_SCALE = 1.0 / (2 * L * SPEC * MIX_UP)

FORWARD = ("even_kv", "odd_v", "even", "odd")
LAG0 = len(FORWARD) * 2 * P
MIX0 = LAG0 + 2 * L
MIXW = L
CONSTS = MIX0 + 4 * MIXW


def constant_table():
    even, even_kv, odd, odd_v, lags, mix_even, mix_odd = spectral_matrices()
    table = np.zeros((P, CONSTS), np.float16)

    def parts(m):
        high = m.astype(np.float16)
        return high, (m - high).astype(np.float16)

    for n, m in enumerate((even_kv, odd_v, even, odd)):
        for part, v in enumerate(parts(m)):
            col = (2 * n + part) * P
            table[:, col:col + P] = np.vstack([v, v])
    for part, v in enumerate(parts(lags)):
        table[:, LAG0 + part * L:LAG0 + (part + 1) * L] = v
    for n, m in enumerate((mix_even, mix_odd)):
        for part, v in enumerate(parts(m)):
            col = MIX0 + (2 * n + part) * MIXW
            table[:, col:col + L] = v
    return table


XT_BANK = (6, 4)
DOWN_PARTS = ((0, 4), (4, 8), (8, 11), (11, 14))


ATTENTION_ALONE = (
    ("kspec", 0), ("stats", 0), ("vspec", 0), ("qspec", 0), ("kspec", 1), ("q_norm", 0), ("k_split", 0),
    ("stats", 1), ("qspec", 1), ("q_split", 0), ("kspec", 2), ("q_norm", 1), ("prod", 0), ("kspec", 3),
    ("qspec", 2), ("vspec", 1), ("vspec", 2), ("k_split", 1), ("k_split", 2), ("k_split", 3), ("kcopy", 0),
    ("q_split", 1), ("kcopy", 1), ("prod", 1), ("psplit", 0), ("prod", 2), ("prod", 3), ("max", 0),
    ("psplit", 1), ("vspec", 3), ("qspec", 3), ("kcopy", 2), ("kcopy", 3), ("max", 1), ("psplit", 2),
    ("lags", 0), ("match", 0), ("psplit", 3), ("vcopy", 0), ("exp", 0), ("exp", 1), ("vcopy", 1), ("lags", 1),
    ("scale", 0), ("lags", 2), ("scale", 1), ("lags", 3), ("match", 1), ("vcopy", 2), ("sum", 0), ("wsplit", 0),
    ("wsplit", 1), ("vcopy", 3), ("wt", 0), ("wt", 1), ("wspec", 0), ("wcopy", 0), ("max", 2), ("scale", 2),
    ("sum", 1), ("max", 3), ("exp", 2), ("scale", 3), ("match", 2), ("match", 3), ("sum", 2), ("wspec", 1),
    ("wt", 2), ("wcopy", 1), ("exp", 3), ("wsplit", 2), ("sum", 3), ("wsplit", 3), ("mix_prod", 0),
    ("mix_prod", 1), ("mix_prod", 2), ("p2split", 0), ("wt", 3), ("p2split", 1), ("wspec", 2), ("mix_prod", 3),
    ("wcopy", 2), ("mix_prod", 4), ("p2split", 2), ("wspec", 3), ("mix_prod", 5), ("p2split", 3),
    ("mix_prod", 6), ("wcopy", 3), ("p2split", 4), ("mix_prod", 7), ("p2split", 5), ("p2split", 6),
    ("p2split", 7), ("mix", 0), ("residual", 0), ("residual", 1), ("xn", 0), ("xsplit", 0), ("mix", 1),
    ("xsplit", 1), ("xt", 0), ("xt", 1), ("xn", 1), ("xcopy", 0), ("xcopy", 1), ("early_gate", 0),
    ("early_up", 0),
)
TURN = (
    ("k_split", 0), ("gate", 0), ("stats", 0), ("stats", 1), ("q_norm", 0), ("k_split", 1), ("kspec", 0),
    ("k_split", 2), ("up", 0), ("q_split", 0), ("vspec", 0), ("kcopy", 0), ("kspec", 1), ("tanh", 0),
    ("q_norm", 1), ("qspec", 0), ("prod", 0), ("qspec", 1), ("kspec", 2), ("kcopy", 1), ("vcopy", 0),
    ("prod", 1), ("psplit", 0), ("psplit", 1), ("gate", 1), ("hidden", 0), ("q_split", 1), ("k_split", 3),
    ("vspec", 1), ("prod", 2), ("up", 1), ("vcopy", 1), ("vspec", 2), ("kcopy", 2), ("prod", 3), ("hidden", 1),
    ("qspec", 2), ("kspec", 3), ("tanh", 1), ("vcopy", 2), ("vspec", 3), ("kcopy", 3), ("max", 0), ("max", 1),
    ("vcopy", 3), ("psplit", 2), ("hsplit", 0), ("qspec", 3), ("match", 0), ("gate", 2), ("lags", 0),
    ("hidden", 2), ("lags", 1), ("lags", 2), ("psplit", 3), ("up", 2), ("gate", 3), ("tanh", 2), ("up", 3),
    ("gate", 4), ("exp", 0), ("wt", 0), ("lags", 3), ("sum", 0), ("hsplit", 1), ("hsplit", 2), ("exp", 1),
    ("scale", 0), ("max", 2), ("match", 1), ("match", 2), ("up", 4), ("gate", 5), ("sum", 1), ("wspec", 0),
    ("wsplit", 0), ("tanh", 3), ("hidden", 3), ("scale", 1), ("scale", 2), ("max", 3), ("match", 3),
    ("wsplit", 1), ("sum", 2), ("wt", 1), ("wcopy", 0), ("hsplit", 3), ("sum", 3), ("hidden", 4), ("up", 5),
    ("tanh", 4), ("mix_prod", 0), ("wt", 2), ("exp", 2), ("exp", 3), ("wsplit", 2), ("scale", 3), ("tanh", 5),
    ("hsplit", 4), ("hidden", 5), ("mix_prod", 1), ("wsplit", 3), ("wcopy", 1), ("hidden", 6), ("mix_prod", 2),
    ("gate", 6), ("up", 6), ("wt", 3), ("wspec", 1), ("p2split", 0), ("wcopy", 2), ("hsplit", 5), ("tanh", 6),
    ("mix_prod", 3), ("down", (0, 0)), ("p2split", 1), ("hsplit", 6), ("mix_prod", 4), ("p2split", 2),
    ("p2split", 3), ("wspec", 2), ("wcopy", 3), ("p2split", 4), ("down", (0, 1)), ("p2split", 5),
    ("p2split", 6), ("mix_prod", 5), ("p2split", 7), ("wspec", 3), ("mix", 0), ("down", (0, 2)),
    ("mix_prod", 6), ("mix_prod", 7), ("down", (0, 3)), ("residual", 0), ("xsplit", 0), ("xn", 0), ("mix", 1),
    ("down", (1, 0)), ("residual", 1), ("down", (1, 1)), ("xsplit", 1), ("xt", 0), ("xn", 1), ("down", (1, 2)),
    ("xt", 1), ("out", 0), ("down", (1, 3)), ("xcopy", 0), ("xcopy", 1), ("early_gate", 0), ("early_up", 0),
    ("out", 1),
)
FFN_ALONE = (
    ("gate", 0), ("tanh", 0), ("hidden", 0), ("up", 0), ("gate", 1), ("up", 1), ("gate", 2), ("tanh", 1),
    ("tanh", 2), ("hidden", 1), ("gate", 3), ("up", 2), ("hsplit", 0), ("up", 3), ("gate", 4), ("gate", 5),
    ("up", 4), ("up", 5), ("tanh", 3), ("hsplit", 1), ("gate", 6), ("tanh", 4), ("hsplit", 2), ("hidden", 2),
    ("hidden", 3), ("up", 6), ("hsplit", 3), ("down", (0, 0)), ("hsplit", 4), ("down", (0, 1)), ("hidden", 4),
    ("down", (0, 2)), ("hidden", 5), ("tanh", 5), ("down", (0, 3)), ("hidden", 6), ("out", 0), ("down", (1, 0)),
    ("hsplit", 5), ("tanh", 6), ("down", (1, 1)), ("out", 1), ("down", (1, 2)), ("hsplit", 6), ("down", (1, 3)),
)


def build(nc, x, ctx, g_xattn, g_ffn, w_gate, w_up, w_down, table, eye, out):
    f32, f16 = mybir.dt.float32, mybir.dt.float16
    ALU = mybir.AluOpType
    ACT = mybir.ActivationFunctionType
    AX = mybir.AxisListType

    def sb(name, shape, dt=f32):
        return nc.alloc_sbuf_tensor(name, shape, dt)

    x_sb = sb("x_sb", [P, PAIRS, D])
    ctx_sb = sb("ctx_sb", [P, B, D])
    wg = sb("wg", [P, KT, M], f16)
    wu = sb("wu", [P, KT, M], f16)
    wd = sb("wd", [P, MT, D], f16)
    consts = sb("consts", [P, CONSTS], f16)
    ident = sb("ident", [P, P], f16)
    minus_half = sb("minus_half", [P, 1])
    gates = sb("gates", [P, 2])
    gates_tanh = sb("gates_tanh", [P, 2])
    scales = sb("scales", [P, 2])

    raw_stats = sb("raw_stats", [P, 2 * QP, 6])
    mean_var = sb("mean_var", [P, 2 * QP, 2])
    var_eps = sb("var_eps", [P, 2 * QP])
    rstd = sb("rstd", [P, 2 * QP])

    normed = sb("normed", [P, QP, D])
    k_high_part = sb("k_high_part", [P, QB, D], f16)
    k_stack = sb("k_stack", [P, QB, D], f16)
    q_stack = sb("q_stack", [P, QB, D], f16)
    kv_spec = sb("kv_spec", [P, QB, 2, D])
    prod = sb("prod", [P, 2, D])
    prod_hi = sb("prod_hi", [P, QB, D], f16)
    prod_lo = sb("prod_lo", [P, QB, D], f16)
    top8 = sb("top8", [P, QB, CH, TOP])
    probs = sb("probs", [P, QB, CH, L])
    expo = sb("expo", [P, QB, CH, L + TOP])
    total = sb("total", [P, QB, CH])
    inv_total = sb("inv_total", [P, QB, CH])
    w_parts = sb("w_parts", [P, QB, CH, 2 * L], f16)
    w_stack = sb("w_stack", [P, QB, D], f16)
    mixed = sb("mixed", [P, 4, D])
    mixed_hi = sb("mixed_hi", [P, QB, 2, D], f16)
    mixed_lo = sb("mixed_lo", [P, QB, 2, D], f16)

    xt_hi = sb("xt_hi", [P, KT, TOK], f16)
    xt_lo = sb("xt_lo", [P, KT, TOK], f16)
    act32 = sb("act32", [P, 2, 2 * TOK])
    hid32 = sb("hid32", [P, 2, 2 * TOK])
    hid_hi = sb("hid_hi", [P, MT, TOK], f16)
    hid_lo = sb("hid_lo", [P, MT, TOK], f16)

    psum = nc.alloc_psum_tensor("psum", [P, 8, 512], f32)

    def k_bank(n, first):
        return 4 + n % 2 if first else 4

    def v_bank(n, first):
        return n if first else 5

    def w_bank(n, m, first):
        return 2 + m if first and n % 2 else 6 + m

    sem = nc.alloc_semaphore

    x_first, x_second, x_more = sem("x_first"), sem("x_second"), sem("x_more")
    ctx_first, ctx_second, ctx_more = sem("ctx_first"), sem("ctx_second"), sem("ctx_more")
    forward_loaded, small_loaded = sem("forward_loaded"), sem("small_loaded")
    inverse_loaded = sem("inverse_loaded")
    gate_loaded, up_loaded, down_loaded = sem("gate_loaded"), sem("up_loaded"), sem("down_loaded")
    const_set = sem("const_set")
    tanh_gates = sem("tanh_gates")
    raw1, stats1, eps1, rstd1 = sem("raw1"), sem("stats1"), sem("eps1"), sem("rstd1")
    raw2, stats2, eps2, rstd2 = sem("raw2"), sem("stats2"), sem("eps2"), sem("rstd2")
    k_high, k_split = sem("k_high"), sem("k_split")
    q_ready, q_high, q_low = sem("q_ready"), sem("q_high"), sem("q_low")
    k_spectra, v_spectra, q_spectra = sem("k_spectra"), sem("v_spectra"), sem("q_spectra")
    k_copied, v_copied = sem("k_copied"), sem("v_copied")
    prod_done, prod_high, prod_low = sem("prod_done"), sem("prod_high"), sem("prod_low")
    lags_done, top8_done, logits_ready = sem("lags_done"), sem("top8_done"), sem("logits_ready")
    exp_done, sum_done, inv_ready = sem("exp_done"), sem("sum_done"), sem("inv_ready")
    probs_ready = sem("probs_ready")
    w_high, w_low, wt_done, w_copied = sem("w_high"), sem("w_low"), sem("wt_done"), sem("w_copied")
    w_spectra = sem("w_spectra")
    mixed_done, mixed_high = sem("mixed_done"), sem("mixed_high")
    mixed_low = (sem("mixed_low_even"), sem("mixed_low_odd"))
    mix_done, x1_ready = sem("mix_done"), sem("x1_ready")
    xn_ready, xn_high, xn_low = sem("xn_ready"), sem("xn_high"), sem("xn_low")
    xt_done, xt_high, xt_low = sem("xt_done"), sem("xt_high"), sem("xt_low")
    gate_done, up_done, tanh_done, silu_done = sem("gate_done"), sem("up_done"), sem("tanh_done"), sem("silu_done")
    hid_done, hid_high, hid_low = sem("hid_done"), sem("hid_high"), sem("hid_low")
    down_done, out_ready, stored = sem("down_done"), sem("out_ready"), sem("stored")

    attention, ffn, both = ATTENTION_ALONE, FFN_ALONE, TURN

    def alone(engine, always_met, count):
        if not isinstance(count, int):
            engine.to_reg(count)
        engine.wait_ge(always_met, 16)

    def forward_column(name, part):
        return (2 * FORWARD.index(name) + part) * P

    def forward(name, part):
        col = forward_column(name, part)
        return consts[:, col:col + P]

    def mix_matrix(n, part):
        col = MIX0 + (2 * n + part) * MIXW
        return consts[:, col:col + L]

    def rows(half):
        return slice(half * L, (half + 1) * L)

    def one(tile, partitions, n):
        return tile[partitions, bass.ds(n, 1), :].rearrange("p a d -> p (a d)")

    with nc.Block() as block:

        @block.sync
        def _(sp):
            xv = x.rearrange("(n p) d -> p n d", p=P)
            cv = ctx.rearrange("(n p) d -> p n d", p=L)
            sp.dma_start(x_sb[:, 0:1, :], xv[:, 0:1, :]).then_inc(x_first, 16)
            sp.dma_start(consts[:, 0:LAG0], table[:, 0:LAG0]).then_inc(forward_loaded, 16)
            sp.dma_start(x_sb[:, 1:QP, :], xv[:, 1:QP, :]).then_inc(x_second, 16)
            for h in range(2):
                sp.dma_start(ctx_sb[rows(h), 2:QB, :], cv[:, 2:QB, :]).then_inc(ctx_second, 16)
            sp.dma_start(consts[:, LAG0:CONSTS], table[:, LAG0:CONSTS]).then_inc(inverse_loaded, 16)
            sp.dma_start(gates[:, 0:1], g_xattn).then_inc(small_loaded, 16)
            sp.dma_start(gates[:, 1:2], g_ffn).then_inc(small_loaded, 16)
            sp.dma_start(ident[:, :], eye).then_inc(small_loaded, 16)
            sp.dma_start(wg[:, :, :], w_gate).then_inc(gate_loaded, 16)
            sp.dma_start(x_sb[:, QP:PAIRS, :], xv[:, QP:PAIRS, :]).then_inc(x_more, 16)
            for h in range(2):
                sp.dma_start(ctx_sb[rows(h), QB:B, :], cv[:, QB:B, :]).then_inc(ctx_more, 16)
            sp.dma_start(wu[:, :, :], w_up).then_inc(up_loaded, 16)
            sp.dma_start(wd[:, :, :], w_down).then_inc(down_loaded, 16)
            outv = out.rearrange("(n p) d -> p n d", p=P)

            with sp.Fori(0, PAIRS) as n:
                sp.wait_ge(out_ready, n + 2)
                sp.dma_start(outv[:, bass.ds(n, 1), :], x_sb[:, bass.ds(n, 1), :]).then_inc(stored, 16)
            sp.wait_ge(stored, 16 * PAIRS)

        @block.gpsimd
        def _(pool):
            nc.gpsimd.memset(minus_half[:, :], -0.5).then_inc(const_set, 1)
            nc.gpsimd.memset(k_high_part[:, :, :], 0.0).then_inc(const_set, 1)
            pool.wait_ge(const_set, 2)

            def reciprocal_std(n, stats_done, eps_done, rstd_done, count):
                alone(pool, x_first, count)
                pool.wait_ge(stats_done, count)
                nc.gpsimd.tensor_scalar_add(var_eps[:, n:n + 1], mean_var[:, n, 1:2], EPS).then_inc(eps_done, 1)
                pool.wait_ge(eps_done, count)
                nc.gpsimd.tensor_tensor(rstd[:, n:n + 1], var_eps[:, n:n + 1], minus_half[:, :],
                                        ALU.pow).then_inc(rstd_done, 1)

            def attention_step(step, n, i, first):
                if step == "stats":
                    reciprocal_std(n, stats1, eps1, rstd1, QP * i + n + 1)
                if step == "k_split":
                    if first and n % 2 == 0:
                        pool.wait_ge((ctx_first, ctx_second)[n // 2], 32)
                    pool.wait_ge(k_high, QB * i + n + 1)
                    if not first and n == 0:
                        pool.wait_ge(v_spectra, QB * i)
                    nc.gpsimd.tensor_tensor(k_stack[:, n, :], one(ctx_sb, slice(0, P), QB * i + n),
                                            k_high_part[:, n, :], ALU.subtract).then_inc(k_split, 1)
                if step == "psplit":
                    pool.wait_ge(prod_high, QB * i + n + 1)
                    nc.gpsimd.tensor_tensor(prod_lo[:, n, :], prod[:, n % 2, :], prod_hi[:, n, :],
                                            ALU.subtract).then_inc(prod_low, 1)
                if step == "scale":
                    pool.wait_ge(inv_ready, QB * i + n + 1)
                    nc.gpsimd.tensor_tensor(probs[:, n, :, :], probs[:, n, :, :],
                                            inv_total[:, n, :].unsqueeze(2).broadcast_to([P, CH, L]),
                                            ALU.mult).then_inc(probs_ready, 1)
                if step == "wsplit":
                    pool.wait_ge(w_high, QB * i + n + 1)
                    nc.gpsimd.tensor_tensor(w_parts[:, n, :, L:2 * L], probs[:, n, :, :],
                                            w_parts[:, n, :, 0:L], ALU.subtract).then_inc(w_low, 1)
                if step == "xsplit":
                    pool.wait_ge(xn_high, QP * i + n + 1)
                    nc.gpsimd.tensor_tensor(prod_hi[:, QP + n, :], normed[:, n, :], prod_hi[:, n, :],
                                            ALU.subtract).then_inc(xn_low, 1)
                if step == "p2split" and not (first and n % 2):
                    b, m = n // 2, n % 2
                    pool.wait_ge(mixed_high, 2 * QB * i + n + 1)
                    nc.gpsimd.tensor_tensor(mixed_lo[:, b, m, :], mixed[:, n % 4, :], mixed_hi[:, b, m, :],
                                            ALU.subtract).then_inc(mixed_low[n % 2], 1)
                if step == "residual":
                    reciprocal_std(QP + n, stats2, eps2, rstd2, QP * i + n + 1)

            def ffn_step(step, n, j):
                if step == "hsplit":
                    pool.wait_ge(hid_high, STEPS * j + n + 1)
                    nc.gpsimd.tensor_tensor(hid_lo[:, 2 * n:2 * n + 2, :].rearrange("p a t -> p (a t)"),
                                            hid32[:, n % 2, :],
                                            hid_hi[:, 2 * n:2 * n + 2, :].rearrange("p a t -> p (a t)"),
                                            ALU.subtract).then_inc(hid_low, 1)

            for step, n in attention:
                attention_step(step, n, 0, True)
            pool.wait_ge(ctx_more, 32)
            with pool.Fori(1, QUADS) as i:
                for step, n in both:
                    attention_step(step, n, i, False)
                    ffn_step(step, n, i - 1)
            for step, n in ffn:
                ffn_step(step, n, QUADS - 1)

        @block.scalar
        def _(act):
            for h in range(2):
                act.dma_start(ctx_sb[rows(h), 0:2, :], ctx.rearrange("(n p) d -> p n d", p=L)[:, 0:2, :])\
                   .then_inc(ctx_first, 16)

            def attention_step(step, n, i, first):
                if step == "k_split":
                    if first and n % 2 == 0:
                        act.wait_ge((ctx_first, ctx_second)[n // 2], 32)
                    if first and n == 0:
                        act.wait_ge(const_set, 2)
                    if not first:
                        act.wait_ge(k_split, QB * (i - 1) + n + 1)
                    nc.scalar.activation(k_high_part[rows(1), n, :], one(ctx_sb, rows(1), QB * i + n),
                                         ACT.Copy).then_inc(k_high, 1)
                if step == "q_split":
                    act.wait_ge(q_ready, QP * i + n + 1)
                    if not first and n == 0:
                        act.wait_ge(q_spectra, QB * i)
                    for h in range(2):
                        last = nc.scalar.activation(q_stack[rows(h), 2 * n + h, :], normed[rows(h), n, :], ACT.Copy)
                    last.then_inc(q_high, 1)
                if step == "kcopy":
                    act.wait_ge(k_spectra, QB * i + n + 1)
                    if not first and n == 0:
                        act.wait_ge(mixed_done, 2 * QB * i)
                    nc.scalar.activation(kv_spec[:, n, 0, :], psum[:, k_bank(n, first), :], ACT.Copy,
                                         scale=SPEC).then_inc(k_copied, 1)
                if step == "vcopy":
                    act.wait_ge(v_spectra, QB * i + n + 1)
                    nc.scalar.activation(kv_spec[:, n, 1, :], psum[:, v_bank(n, first), :], ACT.Copy,
                                         scale=SPEC).then_inc(v_copied, 1)
                if step == "psplit":
                    act.wait_ge(prod_done, QB * i + n + 1)
                    if not first and n == 0:
                        act.wait_ge(xt_done, QP * i)
                    nc.scalar.activation(prod_hi[:, n, :], prod[:, n % 2, :], ACT.Copy).then_inc(prod_high, 1)
                if step == "exp":
                    if first and n == 0:
                        act.wait_ge(small_loaded, 48)
                        nc.scalar.activation(gates_tanh[:, :], gates[:, :], ACT.Tanh).then_inc(tanh_gates, 1)
                    act.wait_ge(logits_ready, QB * i + n + 1)
                    nc.scalar.activation(expo[:, n, :, :], expo[:, n, :, :], ACT.Exp).then_inc(exp_done, 1)
                if step == "wsplit":
                    act.wait_ge(probs_ready, QB * i + n + 1)
                    if not first and n == 0:
                        act.wait_ge(wt_done, QB * i)
                    nc.scalar.activation(w_parts[:, n, :, 0:L], probs[:, n, :, :], ACT.Copy).then_inc(w_high, 1)
                if step == "wcopy":
                    act.wait_ge(wt_done, QB * i + n + 1)
                    if not first and n == 0:
                        act.wait_ge(w_spectra, QB * i)
                    nc.scalar.activation(w_stack[:, n, :], psum[:, 4 + n % 2, :], ACT.Copy).then_inc(w_copied, 1)
                if step == "p2split":
                    b, m = n // 2, n % 2
                    act.wait_ge(mixed_done, 2 * QB * i + n + 1)
                    if not first and n == 0:
                        act.wait_ge(mix_done, QP * i)
                    nc.scalar.activation(mixed_hi[:, b, m, :], mixed[:, n % 4, :], ACT.Copy)\
                      .then_inc(mixed_high, 1)
                if step == "xsplit":
                    act.wait_ge(xn_ready, QP * i + n + 1)
                    nc.scalar.activation(prod_hi[:, n, :], normed[:, n, :], ACT.Copy).then_inc(xn_high, 1)
                if step == "xcopy":
                    act.wait_ge(xt_done, QP * i + n + 1)
                    if not first and n == 0:
                        act.wait_ge(up_done, STEPS * i)
                    nc.scalar.activation(xt_hi[:, :, n * P:(n + 1) * P],
                                         psum[:, XT_BANK[n], :].rearrange("p (k t) -> p k t", k=KT),
                                         ACT.Copy).then_inc(xt_high, 1)

            def ffn_step(step, n, j):
                if step == "tanh":
                    act.wait_ge(gate_done, STEPS * j + n + 1)
                    nc.scalar.activation(act32[:, n % 2, :], psum[:, 2 * (n % 2), :], ACT.Tanh,
                                         scale=0.5).then_inc(tanh_done, 1)
                if step == "hsplit":
                    act.wait_ge(hid_done, STEPS * j + n + 1)
                    nc.scalar.activation(hid_hi[:, 2 * n:2 * n + 2, :].rearrange("p a t -> p (a t)"),
                                         hid32[:, n % 2, :], ACT.Copy).then_inc(hid_high, 1)

            for step, n in attention:
                attention_step(step, n, 0, True)
            act.wait_ge(ctx_more, 32)
            with act.Fori(1, QUADS) as i:
                for step, n in both:
                    attention_step(step, n, i, False)
                    ffn_step(step, n, i - 1)
            for step, n in ffn:
                ffn_step(step, n, QUADS - 1)

        @block.vector
        def _(dve):
            def layer_stats(n, pair, raw_done, stats_done, count):
                nc.vector.bn_stats(raw_stats[:, n, :], one(x_sb, slice(0, P), pair)).then_inc(raw_done, 1)
                alone(dve, x_first, count)
                dve.wait_ge(raw_done, count)
                nc.vector.bn_aggr(mean_var[:, n, :], raw_stats[:, n, :]).then_inc(stats_done, 1)

            def attention_step(step, n, i, first):
                if step == "stats":
                    if first:
                        dve.wait_ge((x_first, x_second)[n], 16)
                    layer_stats(n, QP * i + n, raw1, stats1, QP * i + n + 1)
                if step == "q_norm":
                    dve.wait_ge(rstd1, QP * i + n + 1)
                    if not first and n == 0:
                        dve.wait_ge(xn_low, QP * i)
                    nc.vector.tensor_scalar(normed[:, n, :], one(x_sb, slice(0, P), QP * i + n),
                                            mean_var[:, n, 0:1], rstd[:, n:n + 1],
                                            ALU.subtract, ALU.mult).then_inc(q_ready, 1)
                if step == "q_split":
                    dve.wait_ge(q_high, QP * i + n + 1)
                    for h in range(2):
                        last = nc.vector.tensor_tensor(q_stack[rows(1 - h), 2 * n + h, :], normed[rows(h), n, :],
                                                       q_stack[rows(h), 2 * n + h, :], ALU.subtract)
                    last.then_inc(q_low, 1)
                if step == "prod":
                    dve.wait_ge(q_spectra, QB * i + n + 1)
                    dve.wait_ge(k_copied, QB * i + n + 1)
                    if n >= 2:
                        dve.wait_ge(prod_low, QB * i + n - 1)
                    elif not first:
                        dve.wait_ge(prod_low, QB * i)
                    nc.vector.tensor_tensor(prod[:, n % 2, :], psum[:, 6 + n % 2, :], kv_spec[:, n, 0, :],
                                            ALU.mult).then_inc(prod_done, 1)
                if step == "max":
                    alone(dve, x_first, QB * i + n + 1)
                    dve.wait_ge(lags_done, QB * i + n + 1)
                    corr = psum[:, 4 + n, 0:CH * L].rearrange("p (c l) -> p c l", c=CH)
                    for c in range(CH):
                        last = nc.vector.max(top8[:, n, c, :], corr[:, c, :])
                    last.then_inc(top8_done, 1)
                if step == "match":
                    alone(dve, x_first, QB * i + n + 1)
                    dve.wait_ge(top8_done, QB * i + n + 1)
                    if not first and n == 0:
                        dve.wait_ge(w_low, QB * i)
                    corr = psum[:, 4 + n, 0:CH * L].rearrange("p (c l) -> p c l", c=CH)
                    for c in range(CH):
                        nc.vector.match_replace(probs[:, n, c, :], top8[:, n, c, :], corr[:, c, :], GONE)
                    nc.vector.tensor_tensor(expo[:, n, :, 0:L], corr,
                                            top8[:, n, :, 0:1].broadcast_to([P, CH, L]), ALU.subtract)
                    nc.vector.tensor_tensor(expo[:, n, :, L:L + TOP], top8[:, n, :, :],
                                            top8[:, n, :, 0:1].broadcast_to([P, CH, TOP]),
                                            ALU.subtract).then_inc(logits_ready, 1)
                if step == "sum":
                    dve.wait_ge(exp_done, QB * i + n + 1)
                    nc.vector.tensor_reduce(total[:, n, :], expo[:, n, :, L:L + TOP], AX.X,
                                            ALU.add).then_inc(sum_done, 1)
                    nc.vector.scalar_tensor_tensor(probs[:, n, :, :], probs[:, n, :, :], GONE,
                                                   expo[:, n, :, 0:L], ALU.is_equal, ALU.mult)
                    dve.wait_ge(sum_done, QB * i + n + 1)
                    nc.vector.reciprocal(inv_total[:, n, :], total[:, n, :]).then_inc(inv_ready, 1)
                if step == "mix_prod":
                    b, m = n // 2, n % 2
                    dve.wait_ge(w_spectra, 2 * QB * i + n + 1)
                    if first and m == 1:
                        dve.wait_ge(v_copied, b + 1)
                    if n >= 4:
                        dve.wait_ge(mixed_low[n % 2], QB * i + n // 2 - 1)
                    elif not first:
                        dve.wait_ge(mixed_low[n % 2], QB * i)
                    nc.vector.scalar_tensor_tensor(mixed[:, n % 4, :], psum[:, w_bank(b, m, first), :], MIX_UP,
                                                   kv_spec[:, b, m, :], ALU.mult,
                                                   ALU.mult).then_inc(mixed_done, 1)
                if step == "p2split" and first and n % 2:
                    b, m = n // 2, n % 2
                    dve.wait_ge(mixed_high, n + 1)
                    nc.vector.tensor_tensor(mixed_lo[:, b, m, :], mixed[:, n % 4, :], mixed_hi[:, b, m, :],
                                            ALU.subtract).then_inc(mixed_low[1], 1)
                if step == "residual":
                    if first and n == 0:
                        dve.wait_ge(tanh_gates, 1)
                        nc.vector.tensor_scalar(scales[:, 0:1], gates_tanh[:, 0:1], MIX_SCALE, None, ALU.mult)
                        nc.vector.tensor_scalar(scales[:, 1:2], gates_tanh[:, 1:2], 0.5, None, ALU.mult)\
                          .then_inc(out_ready, 1)
                        dve.wait_ge(out_ready, 1)
                    dve.wait_ge(mix_done, QP * i + n + 1)
                    tokens = one(x_sb, slice(0, P), QP * i + n)
                    nc.vector.scalar_tensor_tensor(tokens, psum[:, 4 + n, :], scales[:, 0:1], tokens,
                                                   ALU.mult, ALU.add).then_inc(x1_ready, 1)
                    alone(dve, x_first, QP * i + n + 1)
                    dve.wait_ge(x1_ready, QP * i + n + 1)
                    layer_stats(QP + n, QP * i + n, raw2, stats2, QP * i + n + 1)
                if step == "xn":
                    dve.wait_ge(rstd2, QP * i + n + 1)
                    nc.vector.tensor_scalar(normed[:, n, :], one(x_sb, slice(0, P), QP * i + n),
                                            mean_var[:, QP + n, 0:1], rstd[:, QP + n:QP + n + 1],
                                            ALU.subtract, ALU.mult).then_inc(xn_ready, 1)
                if step == "xcopy":
                    dve.wait_ge(xt_done, QP * i + n + 1)
                    nc.vector.tensor_copy(xt_lo[:, :, n * P:(n + 1) * P],
                                          psum[:, XT_BANK[n] + 1, :].rearrange("p (k t) -> p k t", k=KT))\
                      .then_inc(xt_low, 1)

            def ffn_step(step, n, j):
                if step == "hidden":
                    gate, up = psum[:, 2 * (n % 2), :], psum[:, 2 * (n % 2) + 1, :]
                    a = act32[:, n % 2, :]
                    dve.wait_ge(tanh_done, STEPS * j + n + 1)
                    nc.vector.scalar_tensor_tensor(a, a, 1.0, gate, ALU.add, ALU.mult).then_inc(silu_done, 1)
                    dve.wait_ge(silu_done, STEPS * j + n + 1)
                    dve.wait_ge(up_done, STEPS * j + n + 1)
                    if n >= 2:
                        dve.wait_ge(hid_low, STEPS * j + n - 1)
                    nc.vector.tensor_tensor(hid32[:, n % 2, :], a, up, ALU.mult).then_inc(hid_done, 1)
                if step == "out":
                    dve.wait_ge(down_done, QP * j + n + 1)
                    tokens = one(x_sb, slice(0, P), QP * j + n)
                    nc.vector.scalar_tensor_tensor(tokens, psum[:, 2 + n, :], scales[:, 1:2], tokens,
                                                   ALU.mult, ALU.add).then_inc(out_ready, 1)

            for step, n in attention:
                attention_step(step, n, 0, True)
            dve.wait_ge(x_more, 16)
            with dve.Fori(1, QUADS) as i:
                for step, n in both:
                    attention_step(step, n, i, False)
                    ffn_step(step, n, i - 1)
            for step, n in ffn:
                ffn_step(step, n, QUADS - 1)

        @block.tensor
        def _(pe):
            def transform(bank, name, stack):
                for part in range(2):
                    last = nc.tensor.matmul(psum[:, bank, :], forward(name, part), stack,
                                            start=(part == 0), stop=(part == 1))
                return last

            def widen(w, bank, n, tokens):
                for a in range(2):
                    m = (2 * n + a) * P
                    for k in range(KT):
                        for part, xt in enumerate((xt_hi, xt_lo)):
                            last = nc.tensor.matmul(psum[:, bank, a * TOK + tokens.start:a * TOK + tokens.stop],
                                                    w[:, k, m:m + P], xt[:, k, tokens],
                                                    start=(k == 0 and part == 0),
                                                    stop=(k == KT - 1 and part == 1))
                return last

            def attention_step(step, n, i, first):
                if step == "kspec":
                    pe.wait_ge(k_split, QB * i + n + 1)
                    last_user = n - 2 if first else n - 1
                    if last_user >= 0:
                        pe.wait_ge(k_copied, QB * i + last_user + 1)
                    elif not first:
                        pe.wait_ge(xt_high, QP * i)
                        pe.wait_ge(xt_low, QP * i)
                    transform(k_bank(n, first), "even_kv", k_stack[:, n, :]).then_inc(k_spectra, 1)
                if step == "qspec":
                    pe.wait_ge(q_low, QP * i + n // 2 + 1)
                    if n >= 2:
                        pe.wait_ge(prod_done, QB * i + n - 1)
                    transform(6 + n % 2, "even", q_stack[:, n, :]).then_inc(q_spectra, 1)
                if step == "vspec":
                    if not first and n > 0:
                        pe.wait_ge(v_copied, QB * i + n)
                    transform(v_bank(n, first), "odd_v", k_stack[:, n, :]).then_inc(v_spectra, 1)
                if step == "lags":
                    if n == 0:
                        pe.wait_ge(prod_done, QB * i + QB)
                        if not first:
                            pe.wait_ge(v_copied, QB * i + QB)
                        else:
                            pe.wait_ge(inverse_loaded, 16)
                    pe.wait_ge(prod_low, QB * i + n + 1)
                    for c in range(CH):
                        o = psum[:, 4 + n, c * L:(c + 1) * L]
                        high = prod_hi[:, n, c * P:(c + 1) * P]
                        low = prod_lo[:, n, c * P:(c + 1) * P]
                        nc.tensor.matmul(o, high, consts[:, LAG0:LAG0 + L], start=True, stop=False)
                        nc.tensor.matmul(o, high, consts[:, LAG0 + L:LAG0 + 2 * L], start=False, stop=False)
                        last = nc.tensor.matmul(o, low, consts[:, LAG0:LAG0 + L], start=False, stop=True)
                    last.then_inc(lags_done, 1)
                if step == "wt":
                    pe.wait_ge(w_low, QB * i + n + 1)
                    if n >= 2:
                        pe.wait_ge(w_copied, QB * i + n - 1)
                    if first and n == 0:
                        pe.wait_ge(small_loaded, 48)
                    for c in range(CH):
                        last = nc.tensor.matmul(psum[:, 4 + n % 2, c * P:(c + 1) * P], w_parts[:, n, c, :],
                                                ident[:, :], start=True, stop=True)
                    last.then_inc(wt_done, 1)
                if step == "wspec":
                    pe.wait_ge(w_copied, QB * i + n + 1)
                    if n == 0:
                        pe.wait_ge(logits_ready, QB * i + QB)
                        if first:
                            pe.wait_ge(v_copied, QB)
                    last_user = n - 2 if first else n - 1
                    for m, name in enumerate(("even", "odd")):
                        if last_user >= 0:
                            pe.wait_ge(mixed_done, 2 * (QB * i + last_user) + m + 1)
                        transform(w_bank(n, m, first), name, w_stack[:, n, :]).then_inc(w_spectra, 1)
                if step == "mix":
                    pe.wait_ge(w_copied, QB * i + QB)
                    for part, data in enumerate((mixed_hi, mixed_lo)):
                        if part == 0:
                            pe.wait_ge(mixed_high, 2 * QB * i + 4 * n + 4)
                        else:
                            pe.wait_ge(mixed_low[0], QB * i + 2 * n + 2)
                            pe.wait_ge(mixed_low[1], QB * i + 2 * n + 2)
                        for m in range(2):
                            for matrix_part in ((0, 1), (0,))[part]:
                                for h in range(2):
                                    last = nc.tensor.matmul(psum[rows(h), 4 + n, :], mix_matrix(m, matrix_part),
                                                            data[:, 2 * n + h, m, :],
                                                            start=(part + m + matrix_part == 0),
                                                            stop=(part + m == 2))
                    last.then_inc(mix_done, 1)
                if step == "xt":
                    pe.wait_ge(xn_low, QP * i + n + 1)
                    if n == 0:
                        pe.wait_ge(mixed_done, 2 * QB * (i + 1))
                    else:
                        pe.wait_ge(x1_ready, QP * i + QP)
                    for part in range(2):
                        for k in range(KT):
                            last = nc.tensor.matmul(psum[:, XT_BANK[n] + part, k * P:(k + 1) * P],
                                                    prod_hi[:, part * QP + n, k * P:(k + 1) * P], ident[:, :],
                                                    start=True, stop=True)
                    last.then_inc(xt_done, 1)
                if step == "early_gate":
                    pe.wait_ge(xt_high, QP * i + 1)
                    pe.wait_ge(xt_low, QP * i + 1)
                    if first:
                        pe.wait_ge(gate_loaded, 16)
                    else:
                        pe.wait_ge(hid_done, STEPS * i)
                    widen(wg, 0, 0, slice(0, P))
                if step == "early_up":
                    if first:
                        pe.wait_ge(up_loaded, 16)
                    widen(wu, 1, 0, slice(0, P))

            def ffn_step(step, n, j):
                if step == "gate":
                    if n == 0:
                        pe.wait_ge(xt_high, QP * j + QP)
                        pe.wait_ge(xt_low, QP * j + QP)
                    elif n == 1:
                        pe.wait_ge(out_ready, QP * j + 1)
                    else:
                        pe.wait_ge(hid_done, STEPS * j + n - 1)
                tokens = slice(P, TOK) if n == 0 else slice(0, TOK)
                if step == "gate":
                    widen(wg, 2 * (n % 2), n, tokens).then_inc(gate_done, 1)
                if step == "up":
                    widen(wu, 2 * (n % 2) + 1, n, tokens).then_inc(up_done, 1)
                if step == "down":
                    p, part_of = n
                    tok = slice(p * P, (p + 1) * P)
                    first_m, end_m = DOWN_PARTS[part_of]
                    if p == 0 and part_of == 0:
                        pe.wait_ge(hid_done, STEPS * j + STEPS - 1)
                    if p == 0:
                        pe.wait_ge(hid_low, STEPS * j + (end_m + 1) // 2)
                    for m in range(first_m, end_m):
                        for part, hid in enumerate((hid_hi, hid_lo)):
                            last = nc.tensor.matmul(psum[:, 2 + p, :], hid[:, m, tok], wd[:, m, :],
                                                    start=(m == 0 and part == 0),
                                                    stop=(m == MT - 1 and part == 1))
                    if end_m == MT:
                        last.then_inc(down_done, 1)

            pe.wait_ge(forward_loaded, 16)
            for step, n in attention:
                attention_step(step, n, 0, True)
            pe.wait_ge(down_loaded, 16)
            with pe.Fori(1, QUADS) as i:
                for step, n in both:
                    attention_step(step, n, i, False)
                    ffn_step(step, n, i - 1)
            for step, n in ffn:
                ffn_step(step, n, QUADS - 1)


def kernel(**inputs):
    import concourse.bacc as bacc
    from concourse.bass_utils import run_bass_kernel_spmd

    def tiles(w, contract):
        return np.ascontiguousarray(np.asarray(w).T.reshape(contract, P, -1).transpose(1, 0, 2))

    arrays = {
        "x": np.ascontiguousarray(np.asarray(inputs["x"]).reshape(B * L, D)),
        "ctx": np.ascontiguousarray(np.asarray(inputs["ctx_4096"]).reshape(B * L, D)),
        "g_xattn": np.ascontiguousarray(np.broadcast_to(np.asarray(inputs["g_xattn"]).reshape(1, 1), (P, 1))),
        "g_ffn": np.ascontiguousarray(np.broadcast_to(np.asarray(inputs["g_ffn"]).reshape(1, 1), (P, 1))),
        "w_gate": tiles(inputs["L0_ffn_W_gate"], KT),
        "w_up": tiles(inputs["L0_ffn_W_up"], KT),
        "w_down": tiles(inputs["L0_ffn_W_down"], MT),
        "table": constant_table(),
        "eye": np.eye(P, dtype=np.float16),
    }
    nc = bacc.Bacc("TRN2", target_bir_lowering=False, num_devices=1)
    args = [nc.dram_tensor(n, a.shape, mybir.dt.from_np(a.dtype), kind="ExternalInput").ap()
            for n, a in arrays.items()]
    out = nc.dram_tensor("out", (B * L, D), mybir.dt.float32, kind="ExternalOutput").ap()
    build(nc, *args, out)
    r = run_bass_kernel_spmd(nc, [arrays], core_ids=[0])
    return r.results[0]["out"].reshape(B, L, D)
```
